# Optimizing a Trainium2 kernel written in Bass

```python
import numpy as np
import jax
import jax.numpy as jnp

def _softmax(x, axis=-1):
    return jax.nn.softmax(x, axis=axis)

def _gelu(x):
    return jax.nn.gelu(x, approximate=True)

def _silu(x):
    return jax.nn.silu(x)

def _sigmoid(x):
    return jax.nn.sigmoid(x)

def _layernorm(x, axis=-1, eps=1e-05):
    m = jnp.mean(x, axis=axis, keepdims=True)
    v = jnp.var(x, axis=axis, keepdims=True)
    return (x - m) / jnp.sqrt(v + eps)

def _scatter_add(tgt, idx, src, axis=0):
    return tgt.at[idx].add(src)

def _segment_sum(src, seg, n):
    return jax.ops.segment_sum(src, seg, n)
kernel_name = 'mk_adaln_ffn_d2_seqx_r8_825364'

def setup_inputs(seed: int=0):
    np.random.seed(seed)
    _w = jnp.asarray

    def _rec_inputs():
        import jax
        import jax.numpy as jnp
        _rk = jax.random.key(seed)
        x = -0.000125 + 0.9999 * jax.random.normal(jax.random.fold_in(_rk, 1), (32, 128, 128), jnp.float32)
        _lenS = 128 - jax.random.randint(jax.random.fold_in(_rk, 7), (32,), 0, max(1, 128 // 4) + 1, jnp.int32)
        _lenS2 = 128 - jax.random.randint(jax.random.fold_in(_rk, 8), (32,), 0, max(1, 128 // 4) + 1, jnp.int32)
        condB_deltat = jax.random.uniform(jax.random.fold_in(_rk, 11), (32,), jnp.float32, 0.0, 1.99976)
        itok_B_0_6 = jax.random.randint(jax.random.fold_in(_rk, 12), (32,), 0, 7, jnp.int32)
        return (x, condB_deltat, itok_B_0_6)
    x, condB_deltat, itok_B_0_6 = _rec_inputs()

    def _L0_cond_setup():
        import jax, jax.numpy as jnp
        import numpy as np
        B, F, T = (32, 64, 128)
        key = jax.random.key(seed)
        k1, k2, k3, k4 = jax.random.split(key, 4)
        x = jax.random.normal(k1, (B, 2 * F, T), dtype=jnp.float32)
        delta_t = jax.random.uniform(k2, (B,), dtype=jnp.float32, minval=0.5, maxval=2.0)
        amplitudes = jax.random.uniform(k3, (F,), dtype=jnp.float32, minval=0.7, maxval=1.3)
        frequencies = jax.random.uniform(k4, (F,), dtype=jnp.float32, minval=0.0, maxval=2.0 * np.pi)
        return {'x': x, 'delta_t': delta_t, 'amplitudes': amplitudes, 'frequencies': frequencies}
    _L0_cond_all = _L0_cond_setup()
    _L0_cond_in = {k: v for k, v in _L0_cond_all.items() if k in ('amplitudes', 'frequencies')}
    del _L0_cond_all

    def _L0_ffn_setup():
        import jax, jax.numpy as jnp
        import numpy as np
        D_MODEL = 128
        key = jax.random.key(seed)
        k_x, k_w, k_a1, k_a2 = jax.random.split(key, 4)
        x = jax.random.normal(k_x, (4, 256, D_MODEL), dtype=jnp.float32)
        weight = jax.random.normal(k_w, (D_MODEL, D_MODEL), dtype=jnp.float32) * 0.02
        aux_weight1 = jax.random.normal(k_a1, (D_MODEL, D_MODEL), dtype=jnp.float32) * 0.02
        aux_weight2 = jax.random.normal(k_a2, (D_MODEL, D_MODEL), dtype=jnp.float32) * 0.02
        bias = jnp.zeros((D_MODEL,), dtype=jnp.float32)
        return {'x': x, 'weight': weight, 'aux_weight1': aux_weight1, 'aux_weight2': aux_weight2, 'bias': bias}
    _L0_ffn_all = _L0_ffn_setup()
    _L0_ffn_in = {k: v for k, v in _L0_ffn_all.items() if k in ('weight', 'aux_weight1', 'aux_weight2', 'bias')}
    del _L0_ffn_all

    def _L1_cond_setup():
        import jax, jax.numpy as jnp
        import numpy as np
        N_PROFILES = 8
        HIDDEN = 128
        BOTTLENECK = 128
        EPS = 1e-05
        key = jax.random.key(seed)
        ks = jax.random.split(key, 8)
        B, S, H, K, P = (16, 256, HIDDEN, BOTTLENECK, N_PROFILES)
        down_w = jax.random.normal(ks[0], (P, H, K), dtype=jnp.float32) * (1.0 / np.sqrt(H))
        down_b = jax.random.normal(ks[1], (P, K), dtype=jnp.float32) * 0.01
        up_w = jax.random.normal(ks[2], (P, K, H), dtype=jnp.float32) * (1.0 / np.sqrt(K))
        up_b = jax.random.normal(ks[3], (P, H), dtype=jnp.float32) * 0.01
        ln_g = jnp.ones((P, H), dtype=jnp.float32)
        ln_b = jnp.zeros((P, H), dtype=jnp.float32)
        hidden = jax.random.normal(ks[4], (B, S, H), dtype=jnp.float32)
        profile_ids = jax.random.randint(ks[5], (B,), 0, P)
        return {'hidden': hidden, 'profile_ids': profile_ids, 'down_w': down_w, 'down_b': down_b, 'up_w': up_w, 'up_b': up_b, 'ln_g': ln_g, 'ln_b': ln_b}
    _L1_cond_all = _L1_cond_setup()
    _L1_cond_in = {k: v for k, v in _L1_cond_all.items() if k in ('down_w', 'down_b', 'up_w', 'up_b', 'ln_g', 'ln_b')}
    del _L1_cond_all

    def _L1_ffn_setup():
        import jax, jax.numpy as jnp
        import numpy as np
        D_MODEL, D_FF, N_EXP = (128, 512, 8)
        key = jax.random.key(seed)
        ks = jax.random.split(key, 8)
        s = lambda fan_in: 1.0 / np.sqrt(fan_in)
        x = jax.random.normal(ks[0], (4, 256, D_MODEL), dtype=jnp.float32)
        Wr = jax.random.uniform(ks[1], (N_EXP, D_MODEL), jnp.float32, -s(D_MODEL), s(D_MODEL))
        br = jax.random.uniform(ks[2], (N_EXP,), jnp.float32, -s(D_MODEL), s(D_MODEL))
        W1 = jax.random.uniform(ks[3], (N_EXP, D_FF, D_MODEL), jnp.float32, -s(D_MODEL), s(D_MODEL))
        b1 = jax.random.uniform(ks[4], (N_EXP, D_FF), jnp.float32, -s(D_MODEL), s(D_MODEL))
        W2 = jax.random.uniform(ks[5], (N_EXP, D_MODEL, D_FF), jnp.float32, -s(D_FF), s(D_FF))
        b2 = jax.random.uniform(ks[6], (N_EXP, D_MODEL), jnp.float32, -s(D_FF), s(D_FF))
        return {'x': x, 'Wr': Wr, 'br': br, 'W1': W1, 'b1': b1, 'W2': W2, 'b2': b2}
    _L1_ffn_all = _L1_ffn_setup()
    _L1_ffn_in = {k: v for k, v in _L1_ffn_all.items() if k in ('Wr', 'br', 'W1', 'b1', 'W2', 'b2')}
    del _L1_ffn_all
    return {'x': x, 'condB_deltat': condB_deltat, 'itok_B_0_6': itok_B_0_6, 'L0_cond_amplitudes': _L0_cond_in['amplitudes'], 'L0_cond_frequencies': _L0_cond_in['frequencies'], 'L0_ffn_weight': _L0_ffn_in['weight'], 'L0_ffn_aux_weight1': _L0_ffn_in['aux_weight1'], 'L0_ffn_aux_weight2': _L0_ffn_in['aux_weight2'], 'L0_ffn_bias': _L0_ffn_in['bias'], 'L1_cond_down_w': _L1_cond_in['down_w'], 'L1_cond_down_b': _L1_cond_in['down_b'], 'L1_cond_up_w': _L1_cond_in['up_w'], 'L1_cond_up_b': _L1_cond_in['up_b'], 'L1_cond_ln_g': _L1_cond_in['ln_g'], 'L1_cond_ln_b': _L1_cond_in['ln_b'], 'L1_ffn_Wr': _L1_ffn_in['Wr'], 'L1_ffn_br': _L1_ffn_in['br'], 'L1_ffn_W1': _L1_ffn_in['W1'], 'L1_ffn_b1': _L1_ffn_in['b1'], 'L1_ffn_W2': _L1_ffn_in['W2'], 'L1_ffn_b2': _L1_ffn_in['b2']}

def reference(x, condB_deltat, itok_B_0_6, L0_cond_amplitudes, L0_cond_frequencies, L0_ffn_weight, L0_ffn_aux_weight1, L0_ffn_aux_weight2, L0_ffn_bias, L1_cond_down_w, L1_cond_down_b, L1_cond_up_w, L1_cond_up_b, L1_cond_ln_g, L1_cond_ln_b, L1_ffn_Wr, L1_ffn_br, L1_ffn_W1, L1_ffn_b1, L1_ffn_W2, L1_ffn_b2):
    import jax
    import jax.numpy as jnp

    def _L0_cond_ref(x, delta_t, amplitudes, frequencies):
        import jax, jax.numpy as jnp
        import numpy as np
        B, F, T = (32, 64, 128)
        Bn = x.shape[0]
        Fn = amplitudes.shape[0]
        a = amplitudes[None, :] ** delta_t[:, None]
        ang = frequencies[None, :] * delta_t[:, None]
        c = a * jnp.cos(ang)
        s = a * jnp.sin(ang)
        xr = x.reshape(Bn, Fn, 2, -1)
        x0, x1 = (xr[:, :, 0], xr[:, :, 1])
        out0 = c[..., None] * x0 - s[..., None] * x1
        out1 = s[..., None] * x0 + c[..., None] * x1
        return jnp.stack([out0, out1], axis=2).reshape(x.shape)

    def _L0_ffn_ref(x, weight, aux_weight1, aux_weight2, bias):
        import jax, jax.numpy as jnp
        import numpy as np
        D_MODEL = 128
        h = jnp.einsum('btc,cd->btd', x, weight)
        h = jnp.einsum('btc,cd->btd', h, aux_weight1)
        h = jnp.einsum('btc,cd->btd', h, aux_weight2)
        return jnp.tanh(h + bias)

    def _L1_cond_ref(hidden, profile_ids, down_w, down_b, up_w, up_b, ln_g, ln_b):
        import jax, jax.numpy as jnp
        import numpy as np
        N_PROFILES = 8
        HIDDEN = 128
        BOTTLENECK = 128
        EPS = 1e-05
        Wd = down_w[profile_ids]
        bd = down_b[profile_ids][:, None]
        Wu = up_w[profile_ids]
        bu = up_b[profile_ids][:, None]
        g = ln_g[profile_ids][:, None]
        b = ln_b[profile_ids][:, None]
        z = jax.nn.relu(jnp.einsum('bsh,bhk->bsk', hidden, Wd) + bd)
        y = hidden + jnp.einsum('bsk,bkh->bsh', z, Wu) + bu
        mu = jnp.mean(y, axis=-1, keepdims=True)
        var = jnp.mean(jnp.square(y - mu), axis=-1, keepdims=True)
        return (y - mu) * jax.lax.rsqrt(var + EPS) * g + b

    def _L1_ffn_ref(x, Wr, br, W1, b1, W2, b2):
        import jax, jax.numpy as jnp
        import numpy as np
        D_MODEL, D_FF, N_EXP = (128, 512, 8)
        B, S, D = x.shape
        xf = x.reshape(-1, D)
        logits = xf @ Wr.T + br
        expert_idx = jnp.argmax(logits, axis=-1)
        h = jax.nn.relu(jnp.einsum('td,efd->etf', xf, W1) + b1[:, None, :])
        y = jnp.einsum('etf,edf->etd', h, W2) + b2[:, None, :]
        out = y[expert_idx, jnp.arange(xf.shape[0])]
        return out.reshape(B, S, D)
    x = x + _L0_ffn_ref(_L0_cond_ref(x, condB_deltat, L0_cond_amplitudes, L0_cond_frequencies), L0_ffn_weight, L0_ffn_aux_weight1, L0_ffn_aux_weight2, L0_ffn_bias)
    x = x + _L1_ffn_ref(_L1_cond_ref(x, itok_B_0_6, L1_cond_down_w, L1_cond_down_b, L1_cond_up_w, L1_cond_up_b, L1_cond_ln_g, L1_cond_ln_b), L1_ffn_Wr, L1_ffn_br, L1_ffn_W1, L1_ffn_b1, L1_ffn_W2, L1_ffn_b2)
    return x

_drawn_inputs = setup_inputs


def setup_inputs(seed=0):
    import zlib

    import numpy as np

    out = dict(_drawn_inputs(seed))
    spreads = {'L0_ffn_bias': (0.0, 0.1), 'L1_cond_ln_g': (1.0, 0.2), 'L1_cond_ln_b': (0.0, 0.1)}
    factors = {'L0_cond_amplitudes': 4.64, 'L1_ffn_b1': 2.859}
    for name, (base, spread) in spreads.items():
        noise = np.random.default_rng([zlib.crc32(name.encode()), seed]).standard_normal(out[name].shape)
        drawn = base * np.exp(spread * noise) if base else spread * noise
        out[name] = jnp.asarray(drawn.astype(out[name].dtype))
    for name, factor in factors.items():
        out[name] = (out[name] * factor).astype(out[name].dtype)
    return out
```

```python
from contextlib import ExitStack

import concourse.bass as bass
from concourse import mybir

P = 128
BATCHES = 32
TOKENS = BATCHES * P
EXPERTS = 8
PROFILES = 8
FF = 512
CHUNKS = FF // P
GB = 4
GROUPS = BATCHES // GB
GN = GB * P
PITCH = TOKENS + P
DUMMY = EXPERTS * PITCH
TILES = TOKENS // P + EXPERTS - 1
ROW = 260
ID = 2 * P
NO_TOKEN = float(1 << 20)
CW = 260
EW = FF + CHUNKS
EPS = 1e-5

F32 = mybir.dt.float32
I32 = mybir.dt.int32
BF16 = mybir.dt.bfloat16
ALU = mybir.AluOpType
ACT = mybir.ActivationFunctionType
AX = mybir.AxisListType

TWO_PI_A, TWO_PI_B, TWO_PI_C = 6.28125, 0.0019340515136718750, 1.2556659146e-06
PI_DOWN = 3.1415925
ROUND = 1.5 * 2.0 ** 23


def adaln_moe(nc, xT, w0, bias0, amp, freq, delta, prof, cond, wr, br, w1, w2, b2, out):
    rows_d = nc.dram_tensor("expert_rows", (DUMMY + P, ROW), F32).ap()
    out_rows = out.rearrange("b s d -> (b s) d")

    with ExitStack() as ctx:
        def sb(name, shape, dt=F32):
            return ctx.enter_context(nc.sbuf_tensor(name, shape, dt))

        def sem(name):
            return ctx.enter_context(nc.semaphore(name))

        w0_s = sb("w0_s", [P, 3, P])
        t1 = sb("t1", [P, P])
        wp = sb("wp", [P, P])
        bias0_s = sb("bias0_s", [P, 1])
        prof_s = sb("prof_s", [1, BATCHES], I32)
        amp_s = sb("amp_s", [P, 1])
        freq_s = sb("freq_s", [P, 1])
        delta_s = sb("delta_s", [P, BATCHES])
        cond_s = sb("cond_s", [P, BATCHES, CW])
        wr_s = sb("wr_s", [P, EXPERTS])
        br_s = sb("br_s", [P, EXPERTS])
        w1_s = sb("w1_s", [P, EXPERTS, EW])
        w2_s = sb("w2_s", [P, EXPERTS, CHUNKS, P])
        b2_s = sb("b2_s", [P, EXPERTS, P])

        ident = sb("ident", [P, P])
        swap = sb("swap", [P, P])
        before = sb("before", [P, P], BF16)
        ones_b = sb("ones_b", [P, P], BF16)
        ones_8 = sb("ones_8", [1, EXPERTS])
        neg_half = sb("neg_half", [P, GB])
        falling = sb("falling", [P, GB, EXPERTS])
        area = sb("area", [P, EXPERTS])
        tau = sb("tau", [1, TILES])
        tau128 = sb("tau128", [1, TILES])
        pad = sb("pad", [P, ROW])

        trig = sb("trig", [P, 8, BATCHES])
        ang, turns, red, cosr, sin_t, cos_t, amp_t, amp_b = (trig[:, i, :] for i in range(8))
        cs = sb("cs", [P, 2, BATCHES])
        rot_c = sb("rot_c", [P, 2, GB, P])
        rot = sb("rot", [P, 2, GB, P])

        x1T = sb("x1T", [P, GROUPS, GN])
        u = sb("u", [P, 2, GN])
        tanh_s = sb("tanh_s", [P, 2, GN])
        zT = sb("zT", [P, 2, GN])
        yT = sb("yT", [P, 2, GN])
        yhat = sb("yhat", [P, 2, GN])
        xnT = sb("xnT", [P, 2, GN])
        stats = sb("stats", [P, 2, GB, 6])
        mv = sb("mv", [P, 2, GB, 2])
        vareps = sb("vareps", [P, 2, GB])
        rstd = sb("rstd", [P, 2, GB])
        payload = sb("payload", [P, BATCHES, ROW])

        logits = sb("logits", [P, GB, EXPERTS])
        top = sb("top", [P, GB])
        tied = sb("tied", [P, GB, EXPERTS])
        first = sb("first", [P, GB])
        onehot = sb("onehot", [P, 2, GB, EXPERTS], BF16)
        seen = sb("seen", [P, 2, EXPERTS], BF16)
        groupsum = sb("groupsum", [P, EXPERTS])
        place = sb("place", [P, GB, EXPERTS])
        slot = sb("slot", [P, BATCHES], I32)

        cnt = sb("cnt", [1, EXPERTS])
        cnt_i = sb("cnt_i", [1, EXPERTS], I32)
        nt_i = sb("nt_i", [1, EXPERTS], I32)
        nt = sb("nt", [1, EXPERTS])
        cum = sb("cum", [1, EXPERTS])
        step = sb("step", [1, EXPERTS])
        past = sb("past", [1, TILES, EXPERTS])
        pastw = sb("pastw", [1, TILES, EXPERTS])
        tsum = sb("tsum", [1, TILES])
        pad_row = sb("pad_row", [1, EXPERTS], I32)
        tile_e = sb("tile_e", [1, TILES], I32)
        tile_r = sb("tile_r", [1, TILES], I32)

        rows = sb("rows", [P, 3, ROW])
        ids = sb("ids", [P, 6], I32)
        zero_i = sb("zero_i", [P, 1], I32)
        tileT = sb("tileT", [P, 3, P])
        stage = sb("stage", [P, 3, EW])
        hT = sb("hT", [P, 3, FF])
        resid = sb("resid", [P, 3, P])
        res = sb("res", [P, 3, P])

        bank = [ctx.enter_context(nc.psum_tensor(f"bank{i}", [P, GN], F32)) for i in range(8)]
        ps_u, ps_h, ps_z, ps_y, ps_yr, ps_nT, ps_nr, ps_r = bank
        ps_x1 = ps_u
        ps_log = ps_r[:, 0:GB * EXPERTS]
        ps_pre = ps_r[:, 64:64 + GB * EXPERTS]
        ps_cnt = ps_r[:, 128:128 + EXPERTS]
        ps_t = bank[7]
        ps_lo, ps_hi = bank[0], bank[1]
        ps_out = bank[3:6]

        d_w0 = sem("d_w0")
        d_trig = sem("d_trig")
        d_prof = sem("d_prof")
        d_small = sem("d_small")
        d_x = [sem(f"d_x{g}") for g in range(GROUPS)]
        d_cond = [sem(f"d_cond{g}") for g in range(GROUPS)]
        d_experts = sem("d_experts")
        d_scatter = sem("d_scatter")
        d_pads = sem("d_pads")
        d_dummy = sem("d_dummy")
        d_rows = [sem(f"d_rows{k}") for k in range(3)]
        d_res = [sem(f"d_res{k}") for k in range(3)]

        s_const = sem("s_const")
        s_t1 = sem("s_t1")
        s_t1c = sem("s_t1c")
        s_wp = sem("s_wp")
        s_wpc = sem("s_wpc")
        s_chain = sem("s_chain")
        s_red = sem("s_red")
        s_amp = sem("s_amp")
        s_sin = sem("s_sin")
        s_rotc = sem("s_rotc")
        s_rot = sem("s_rot")
        s_u = sem("s_u")
        s_uc = sem("s_uc")
        s_h = sem("s_h")
        s_tanh = sem("s_tanh")
        s_x1T = sem("s_x1T")
        s_x1 = sem("s_x1")
        s_x1c = sem("s_x1c")
        s_z = sem("s_z")
        s_zc = sem("s_zc")
        s_y = sem("s_y")
        s_yc = sem("s_yc")
        s_yr = sem("s_yr")
        s_stats = sem("s_stats")
        s_mv = sem("s_mv")
        s_var = sem("s_var")
        s_rstd = sem("s_rstd")
        s_yhat = sem("s_yhat")
        s_nT = sem("s_nT")
        s_nTc = sem("s_nTc")
        s_nr = sem("s_nr")
        s_nrc = sem("s_nrc")
        s_log = sem("s_log")
        s_route = sem("s_route")
        s_onehot = sem("s_onehot")
        s_seen = sem("s_seen")
        s_pre = sem("s_pre")
        s_slot = sem("s_slot")
        s_cnt = sem("s_cnt")
        s_padrow = sem("s_padrow")
        s_table = sem("s_table")
        s_tiles = sem("s_tiles")
        s_tT = sem("s_tT")
        s_tTc = sem("s_tTc")
        s_stage = sem("s_stage")
        s_hlo = sem("s_hlo")
        s_hhi = sem("s_hhi")
        s_hloc = sem("s_hloc")
        s_hhic = sem("s_hhic")
        s_out = sem("s_out")
        s_res = sem("s_res")
        s_taken = sem("s_taken")

        N_CONST = 18
        N_ALL = N_CONST + 1
        block = ctx.enter_context(nc.Block())

        def cols(b):
            return slice(b % GB * P, b % GB * P + P)

        def in_turn(lags):
            for t in range(min(lags.values()), GROUPS + max(lags.values())):
                for stage_name, lag in lags.items():
                    if 0 <= t - lag < GROUPS:
                        yield stage_name, t - lag

        @block.sync
        def _(sp):
            sp.dma_start(delta_s[:, :], delta.partition_broadcast(P)).then_inc(d_trig, 16)
            sp.dma_start(freq_s[:, :], freq.rearrange("(p a) -> p a", a=1)).then_inc(d_trig, 16)
            sp.dma_start(amp_s[:, :], amp.rearrange("(p a) -> p a", a=1)).then_inc(d_trig, 16)
            sp.dma_start(x1T[:, 0, :], xT[:, 0:GN]).then_inc(d_x[0], 16)
            sp.dma_start(prof_s[:, :], prof.rearrange("(a n) -> a n", a=1)).then_inc(d_prof, 16)
            sp.dma_start(x1T[:, 1, :], xT[:, GN:2 * GN]).then_inc(d_x[1], 16)
            sp.wait_ge(d_prof, 16)
            for g in range(GROUPS):
                for b in range(g * GB, g * GB + GB):
                    p = sp.value_load(prof_s[0:1, b:b + 1], min_val=0, max_val=PROFILES - 1)
                    sp.dma_start(cond_s[:, b, :], cond[bass.ds(p, 1), :, :].rearrange("a p c -> (a p) c"))\
                        .then_inc(d_cond[g], 16)
                if g + 2 < GROUPS:
                    sp.dma_start(x1T[:, g + 2, :], xT[:, (g + 2) * GN:(g + 3) * GN]).then_inc(d_x[g + 2], 16)
            sp.dma_start(w1_s[:, :, :], w1).then_inc(d_experts, 16)
            sp.dma_start(w2_s[:, :, :, :], w2).then_inc(d_experts, 16)

            sp.wait_ge(s_padrow, 1)
            for e in range(EXPERTS // 2):
                r = sp.value_load(pad_row[0:1, e:e + 1], min_val=0, max_val=DUMMY - P)
                sp.dma_start(rows_d[bass.ds(r, P), :], pad[:, :]).then_inc(d_pads, 16)

            def load_rows(k, r_at):
                r = sp.value_load(tile_r[0:1, r_at], min_val=0, max_val=DUMMY)
                sp.dma_start(rows[:, k, :], rows_d[bass.ds(r, P), :]).then_inc(d_rows[k], 16)

            sp.wait_ge(s_tiles, 1)
            sp.wait_ge(d_scatter, 16 * BATCHES)
            sp.wait_ge(d_pads, 16 * EXPERTS)
            sp.wait_ge(d_dummy, 16)
            for t in range(3):
                load_rows(t, slice(t, t + 1))
            with sp.Fori(0, TILES // 3 - 1) as j:
                for k in range(3):
                    sp.wait_ge(s_tT, j * 3 + (k + 1))
                    sp.wait_ge(s_taken, j * 3 + (k + 1))
                    load_rows(k, bass.ds(j * 3 + (k + 3), 1))

        @block.gpsimd
        def _(pool):
            pool.memset(ident[:, :], 0.0).then_inc(s_const, 1)
            pool.memset(swap[:, :], 0.0).then_inc(s_const, 1)
            pool.memset(pad[:, :], 0.0).then_inc(s_const, 1)
            pool.memset(before[:, :], 1.0).then_inc(s_const, 1)
            pool.memset(ones_b[:, :], 1.0).then_inc(s_const, 1)
            pool.memset(neg_half[:, :], -0.5).then_inc(s_const, 1)
            pool.wait_ge(s_const, 6)
            pool.affine_select(out=ident[:, :], in_=ident[:, :], compare_op=ALU.not_equal, fill=1.0, base=0,
                               pattern=[[-1, P]], channel_multiplier=1).then_inc(s_const, 1)
            pairs = swap[:, :].rearrange("p (f two) -> p f two", two=2)
            pool.affine_select(out=pairs[:, :, 0], in_=pairs[:, :, 0], compare_op=ALU.not_equal, fill=-1.0,
                               base=-1, pattern=[[-2, P // 2]], channel_multiplier=1).then_inc(s_const, 1)
            pool.affine_select(out=pairs[:, :, 1], in_=pairs[:, :, 1], compare_op=ALU.not_equal, fill=1.0,
                               base=0, pattern=[[-2, P // 2]], channel_multiplier=1).then_inc(s_const, 1)
            pool.wait_ge(d_trig, 48)
            pool.wait_ge(s_chain, 1)
            pool.tensor_tensor(amp_t, amp_b, delta_s[:, :], ALU.pow).then_inc(s_amp, 1)
            pool.affine_select(out=before[:, :], in_=before[:, :], compare_op=ALU.is_gt, fill=0.0, base=0,
                               pattern=[[1, P]], channel_multiplier=-1).then_inc(s_const, 1)
            pool.memset(pad[:, ID:ID + 1].bitcast(I32), int(NO_TOKEN)).then_inc(s_const, 1)
            pool.iota(falling[:, :, :], pattern=[[0, GB], [-1, EXPERTS]], base=EXPERTS, channel_multiplier=0,
                      allow_small_or_imprecise_dtypes=True).then_inc(s_const, 1)
            pool.iota(area[:, :], pattern=[[PITCH, EXPERTS]], base=0, channel_multiplier=0,
                      allow_small_or_imprecise_dtypes=True).then_inc(s_const, 1)
            pool.iota(tau[:, :], pattern=[[1, TILES]], base=0, channel_multiplier=0,
                      allow_small_or_imprecise_dtypes=True).then_inc(s_const, 1)
            pool.iota(tau128[:, :], pattern=[[P, TILES]], base=0, channel_multiplier=0,
                      allow_small_or_imprecise_dtypes=True).then_inc(s_const, 1)
            pool.memset(payload[:, :, ID:ROW], 0.0).then_inc(s_const, 1)
            pool.memset(ones_8[:, :], 1.0).then_inc(s_const, 1)
            pool.memset(zero_i[:, :], 0).then_inc(s_const, 1)
            pool.wait_ge(s_const, N_CONST)
            pool.iota(payload[:, :, ID].bitcast(I32), pattern=[[P, BATCHES]], base=0, channel_multiplier=1)\
                .then_inc(s_const, 1)
            pool.dma_start(rows_d[DUMMY:DUMMY + P, :], pad[:, :]).then_inc(d_dummy, 16)

            def cos_part(g):
                if g >= 2:
                    pool.wait_ge(s_rot, g - 1)
                for i in range(GB):
                    b = g * GB + i
                    op = pool.tensor_scalar(rot_c[:, g % 2, i, :], ident[:, :], cs[:, 0, b:b + 1], None, ALU.mult)
                op.then_inc(s_rotc, 1)

            def add_x(g):
                pool.wait_ge(s_tanh, g + 1)
                pool.wait_ge(s_u, g + 1)
                pool.tensor_tensor(x1T[:, g, :], x1T[:, g, :], tanh_s[:, g % 2, :], ALU.add).then_inc(s_x1T, 1)

            def deviation(g):
                pool.wait_ge(s_mv, g + 1)
                pool.tensor_scalar(vareps[:, g % 2, :], mv[:, g % 2, :, 1], EPS, None, ALU.add).then_inc(s_var, 1)
                pool.wait_ge(s_var, g + 1)
                pool.tensor_tensor(rstd[:, g % 2, :], vareps[:, g % 2, :], neg_half[:, :], ALU.pow)\
                    .then_inc(s_rstd, 1)

            def scatter(g):
                pool.wait_ge(s_slot, g + 1)
                pool.wait_ge(s_nrc, g + 1)
                pool.wait_ge(s_x1c, g + 1)
                pool.wait_ge(s_const, N_ALL)
                for b in range(g * GB, g * GB + GB):
                    pool.indirect_dma_start(
                        out=rows_d, out_offset=bass.IndirectOffsetOnAxis(ap=slot[:, b:b + 1], axis=0),
                        in_=payload[:, b, :], in_offset=None).then_inc(d_scatter, 16)

            pool.wait_ge(s_chain, 9)
            for stage_name, g in in_turn({"cos": -2, "dev": 3, "add": 0, "scatter": 5}):
                {"cos": cos_part, "add": add_x, "dev": deviation, "scatter": scatter}[stage_name](g)

            pool.wait_ge(s_tiles, 1)
            pool.wait_ge(d_small, 16 * 4)
            last_token = pool.to_reg(TOKENS - 1)

            def take_rows(k, i, e_at, arrivals):
                e = pool.value_load(tile_e[0:1, e_at], min_val=0, max_val=EXPERTS - 1)
                b2_e = b2_s[:, bass.ds(e, 1), :].rearrange("p a d -> p (a d)")
                pool.wait_ge(d_rows[k], arrivals)
                pool.tensor_tensor(ids[:, i:i + 1], rows[:, k, ID:ID + 1].bitcast(I32), zero_i[:, :], ALU.add)
                pool.tensor_tensor(resid[:, k, :], rows[:, k, P:2 * P], b2_e, ALU.add).then_inc(s_taken, 1)

            def store(k, i):
                pool.indirect_dma_start(
                    out=out_rows, out_offset=bass.IndirectOffsetOnAxis(ap=ids[:, i:i + 1], axis=0),
                    in_=res[:, k, :], in_offset=None, bounds_check=last_token, oob_is_err=False)\
                    .then_inc(d_res[k], 16)

            for t in range(3):
                if t >= 2:
                    pool.wait_ge(s_res, t - 1)
                    pool.wait_ge(s_taken, t)
                take_rows(t, t, slice(t, t + 1), 16)
                if t >= 2:
                    store(t - 2, t - 2)
            with pool.Fori(0, (TILES - 3) // 6) as j:
                for q in range(6):
                    pool.wait_ge(s_res, j * 6 + (q + 2))
                    pool.wait_ge(s_taken, j * 6 + (q + 3))
                    take_rows(q % 3, (q + 3) % 6, bass.ds(j * 6 + (q + 3), 1), j * 32 + 16 * (q // 3 + 2))
                    store((q + 1) % 3, (q + 1) % 6)
            for t in range(TILES - 2, TILES):
                pool.wait_ge(s_res, t + 1)
                pool.wait_ge(s_taken, t + 1)
                store(t % 3, t % 6)
            for k in range(3):
                pool.wait_ge(d_res[k], 16 * (TILES // 3))

        @block.scalar
        def _(act):
            act.dma_start(w0_s[:, :, :], w0).then_inc(d_w0, 16)
            act.dma_start(bias0_s[:, :], bias0.rearrange("(p a) -> p a", a=1)).then_inc(d_small, 16)
            act.dma_start(wr_s[:, :], wr).then_inc(d_small, 16)
            act.dma_start(br_s[:, :], br.partition_broadcast(P)).then_inc(d_small, 16)
            act.dma_start(b2_s[:, :, :].rearrange("p e d -> p (e d)"),
                          b2.rearrange("e d -> (e d)").partition_broadcast(P)).then_inc(d_small, 16)
            act.wait_ge(s_chain, 7)
            nc.scalar.activation(sin_t, red, ACT.Sin).then_inc(s_sin, 1)
            nc.scalar.activation(cos_t, cosr, ACT.Sin).then_inc(s_sin, 1)

            def copy_u(g):
                act.wait_ge(s_u, g + 1)
                if g >= 2:
                    act.wait_ge(s_h, g - 1)
                nc.scalar.activation(u[:, g % 2, :], ps_u[:, :], ACT.Copy).then_inc(s_uc, 1)

            def tanh(g):
                act.wait_ge(s_h, g + 1)
                if g >= 2:
                    act.wait_ge(s_x1T, g - 1)
                nc.scalar.activation(tanh_s[:, g % 2, :], ps_h[:, :], ACT.Tanh, bias=bias0_s[:, 0:1])\
                    .then_inc(s_tanh, 1)

            def copy_x1(g):
                act.wait_ge(s_x1, g + 1)
                nc.scalar.activation(payload[:, g * GB:(g + 1) * GB, P:2 * P],
                                     ps_x1[:, :].rearrange("p (b d) -> p b d", b=GB), ACT.Copy).then_inc(s_x1c, 1)

            def relu_z(g):
                act.wait_ge(s_z, g + 1)
                if g >= 2:
                    act.wait_ge(s_y, g - 1)
                for b in range(g * GB, g * GB + GB):
                    op = nc.scalar.activation(zT[:, g % 2, cols(b)], ps_z[:, cols(b)], ACT.Relu,
                                              bias=cond_s[:, b, 2 * P:2 * P + 1])
                op.then_inc(s_zc, 1)

            def gain(g):
                act.wait_ge(s_nT, g + 1)
                if g >= 2:
                    act.wait_ge(s_log, g - 1)
                for b in range(g * GB, g * GB + GB):
                    op = nc.scalar.activation(xnT[:, g % 2, cols(b)], ps_nT[:, cols(b)], ACT.Identity,
                                              scale=cond_s[:, b, 2 * P + 2:2 * P + 3],
                                              bias=cond_s[:, b, 2 * P + 3:2 * P + 4])
                op.then_inc(s_nTc, 1)

            def copy_xn(g):
                act.wait_ge(s_nr, g + 1)
                nc.scalar.activation(payload[:, g * GB:(g + 1) * GB, 0:P],
                                     ps_nr[:, :].rearrange("p (b d) -> p b d", b=GB), ACT.Copy).then_inc(s_nrc, 1)

            act.wait_ge(d_small, 64)
            for stage_name, g in in_turn({"u": 0, "gain": 4, "tanh": 0, "x1": 1, "z": 1, "xn": 4}):
                if stage_name == "z":
                    act.wait_ge(d_cond[g], 16 * GB)
                {"u": copy_u, "tanh": tanh, "x1": copy_x1, "z": relu_z, "gain": gain, "xn": copy_xn}[stage_name](g)

            act.wait_ge(s_padrow, 1)
            for e in range(EXPERTS // 2, EXPERTS):
                r = act.value_load(pad_row[0:1, e:e + 1], min_val=0, max_val=DUMMY - P)
                act.dma_start(rows_d[bass.ds(r, P), :], pad[:, :]).then_inc(d_pads, 16)

            def copy_tile(k, tiles_done):
                act.wait_ge(s_tT, tiles_done)
                nc.scalar.activation(tileT[:, k, :], ps_t[:, k * P:(k + 1) * P], ACT.Copy).then_inc(s_tTc, 1)

            def relu_lo(k, tiles_done):
                act.wait_ge(s_hlo, tiles_done)
                for c in range(CHUNKS // 2):
                    op = nc.scalar.activation(hT[:, k, c * P:(c + 1) * P], ps_lo[:, c * P:(c + 1) * P],
                                              ACT.Relu, bias=stage[:, k, FF + c:FF + c + 1])
                op.then_inc(s_hloc, 1)

            copy_tile(0, 1)
            relu_lo(0, 1)
            copy_tile(1, 2)
            with act.Fori(0, TILES // 3 - 1) as j:
                for k in range(3):
                    relu_lo((k + 1) % 3, j * 3 + (k + 2))
                    copy_tile((k + 2) % 3, j * 3 + (k + 3))
            relu_lo((TILES - 2) % 3, TILES - 1)
            copy_tile((TILES - 1) % 3, TILES)
            relu_lo((TILES - 1) % 3, TILES)

        @block.tensor
        def _(pe):
            pe.wait_ge(d_w0, 16)
            nc.tensor.matmul(ps_u[:, 0:P], w0_s[:, 1, :], w0_s[:, 2, :], start=True, stop=True).then_inc(s_t1, 1)
            pe.wait_ge(s_t1c, 1)
            nc.tensor.matmul(ps_h[:, 0:P], w0_s[:, 0, :], t1[:, :], start=True, stop=True).then_inc(s_wp, 1)
            pe.wait_ge(s_wpc, 1)
            pe.wait_ge(s_const, 9)

            def mul_w(g):
                pe.wait_ge(d_x[g], 16)
                if g >= 1:
                    pe.wait_ge(s_uc, g)
                if g >= 2:
                    pe.wait_ge(s_x1c, g - 1)
                for i in range(GB):
                    op = nc.tensor.matmul(ps_u[:, i * P:(i + 1) * P], x1T[:, g, i * P:(i + 1) * P], wp[:, :],
                                          start=True, stop=True)
                op.then_inc(s_u, 1)

            def rotate(g):
                pe.wait_ge(s_uc, g + 1)
                pe.wait_ge(s_rot, g + 1)
                if g >= 1:
                    pe.wait_ge(s_tanh, g)
                for i in range(GB):
                    op = nc.tensor.matmul(ps_h[:, i * P:(i + 1) * P], u[:, g % 2, i * P:(i + 1) * P],
                                          rot[:, g % 2, i, :], start=True, stop=True)
                op.then_inc(s_h, 1)

            def turn_x1(g):
                pe.wait_ge(s_x1T, g + 1)
                if g >= 1:
                    pe.wait_ge(s_x1c, g)
                pe.wait_ge(s_uc, min(g + 2, GROUPS))
                for i in range(GB):
                    op = nc.tensor.transpose(ps_x1[:, i * P:(i + 1) * P], x1T[:, g, i * P:(i + 1) * P], ident[:, :])
                op.then_inc(s_x1, 1)

            def down(g):
                pe.wait_ge(d_cond[g], 16 * GB)
                if g >= 1:
                    pe.wait_ge(s_zc, g)
                for b in range(g * GB, g * GB + GB):
                    op = nc.tensor.matmul(ps_z[:, cols(b)], cond_s[:, b, 0:P], x1T[:, g, cols(b)],
                                          start=True, stop=True)
                op.then_inc(s_z, 1)

            def up(g):
                pe.wait_ge(s_zc, g + 1)
                if g >= 1:
                    pe.wait_ge(s_yc, g)
                for b in range(g * GB, g * GB + GB):
                    op = nc.tensor.matmul(ps_y[:, cols(b)], cond_s[:, b, P:2 * P], zT[:, g % 2, cols(b)],
                                          start=True, stop=True)
                op.then_inc(s_y, 1)

            def turn_y(g):
                pe.wait_ge(s_yc, g + 1)
                if g >= 1:
                    pe.wait_ge(s_yhat, g)
                for i in range(GB):
                    op = nc.tensor.transpose(ps_yr[:, i * P:(i + 1) * P], yT[:, g % 2, i * P:(i + 1) * P],
                                             ident[:, :])
                op.then_inc(s_yr, 1)

            def turn_yhat(g):
                pe.wait_ge(s_yhat, g + 1)
                if g >= 1:
                    pe.wait_ge(s_nTc, g)
                for i in range(GB):
                    op = nc.tensor.transpose(ps_nT[:, i * P:(i + 1) * P], yhat[:, g % 2, i * P:(i + 1) * P],
                                             ident[:, :])
                op.then_inc(s_nT, 1)

            def route(g):
                pe.wait_ge(s_nTc, g + 1)
                if g >= 1:
                    pe.wait_ge(s_slot, g)
                    pe.wait_ge(s_nrc, g)
                for i in range(GB):
                    op = nc.tensor.transpose(ps_nr[:, i * P:(i + 1) * P], xnT[:, g % 2, i * P:(i + 1) * P],
                                             ident[:, :])
                op.then_inc(s_nr, 1)
                for i in range(GB):
                    op = nc.tensor.matmul(ps_log[:, i * EXPERTS:(i + 1) * EXPERTS],
                                          xnT[:, g % 2, i * P:(i + 1) * P], wr_s[:, :], start=True, stop=True)
                op.then_inc(s_log, 1)

            def prefix(g):
                pe.wait_ge(s_onehot, g + 1)
                pe.wait_ge(s_const, N_CONST)
                if g >= 1:
                    pe.wait_ge(s_slot, g)
                oh = onehot[:, g % 2, :, :].rearrange("p b e -> p (b e)")
                nc.tensor.matmul(ps_pre, before[:, :], oh, start=True, stop=False, skip_group_check=True)
                for back in range(1, GB):
                    n = (GB - back) * EXPERTS
                    nc.tensor.matmul(ps_pre[:, back * EXPERTS:], ones_b[:, :], oh[:, 0:n], start=False, stop=False,
                                     skip_group_check=True)
                pe.wait_ge(s_seen, g + 1)
                for i in range(GB):
                    op = nc.tensor.matmul(ps_pre[:, i * EXPERTS:(i + 1) * EXPERTS], ones_b[:, :],
                                          seen[:, g % 2, :], start=False, stop=(i == GB - 1),
                                          skip_group_check=True)
                op.then_inc(s_pre, 1)

            pe.wait_ge(d_small, 64)
            steps = {"u": mul_w, "up": up, "h": rotate, "prefix": prefix, "yr": turn_y, "x1": turn_x1, "z": down,
                     "nT": turn_yhat, "route": route}
            for stage_name, g in in_turn({"yr": 3, "u": 0, "nT": 4, "up": 2, "prefix": 5, "h": 0, "x1": 1, "z": 1,
                                          "route": 4}):
                steps[stage_name](g)
            pe.wait_ge(s_seen, GROUPS + 1)
            pe.wait_ge(s_slot, GROUPS)
            nc.tensor.matmul(ps_cnt, ones_b[:, :], seen[:, GROUPS % 2, :], start=True, stop=True).then_inc(s_cnt, 1)

            def turn_tile(k, arrivals):
                pe.wait_ge(d_rows[k], arrivals)
                nc.tensor.transpose(ps_t[:, k * P:(k + 1) * P], rows[:, k, 0:P], ident[:, :]).then_inc(s_tT, 1)

            def hidden(k, tiles_ready, read=None):
                pe.wait_ge(s_stage, tiles_ready)
                pe.wait_ge(s_tTc, tiles_ready)
                for half, used, done in ((ps_lo, s_hloc, s_hlo), (ps_hi, s_hhic, s_hhi)):
                    if read is not None:
                        pe.wait_ge(used, read)
                    for c in range(CHUNKS // 2) if half is ps_lo else range(CHUNKS // 2, CHUNKS):
                        op = nc.tensor.matmul(half[:, c * P:(c + 1) * P], stage[:, k, c * P:(c + 1) * P],
                                              tileT[:, k, :], start=True, stop=True)
                    op.then_inc(done, 1)

            def output(k, e_at, tiles_ready, freed=None):
                e = pe.value_load(tile_e[0:1, e_at], min_val=0, max_val=EXPERTS - 1)
                pe.wait_ge(s_hloc, tiles_ready)
                pe.wait_ge(s_hhic, tiles_ready)
                if freed is not None:
                    pe.wait_ge(s_res, freed)
                for c in range(CHUNKS):
                    w2_e = w2_s[:, bass.ds(e, 1), c, :].rearrange("p a d -> p (a d)")
                    op = nc.tensor.matmul(ps_out[k][:, 0:P], hT[:, k, c * P:(c + 1) * P], w2_e,
                                          start=(c == 0), stop=(c == CHUNKS - 1))
                op.then_inc(s_out, 1)

            pe.wait_ge(s_tiles, 1)
            pe.wait_ge(s_nrc, GROUPS)
            pe.wait_ge(s_x1c, GROUPS)
            turn_tile(0, 16)
            hidden(0, 1)
            turn_tile(1, 16)
            hidden(1, 2, 1)
            turn_tile(2, 16)
            output(0, slice(0, 1), 1)
            hidden(2, 3, 2)
            turn_tile(0, 32)
            output(1, slice(1, 2), 2)
            hidden(0, 4, 3)
            turn_tile(1, 32)
            output(2, slice(2, 3), 3)
            with pe.Fori(1, TILES // 3 - 1) as j:
                for k in range(3):
                    hidden((k + 1) % 3, j * 3 + (k + 2), j * 3 + (k + 1))
                    turn_tile((k + 2) % 3, j * 16 + (16 if k == 0 else 32))
                    output(k, bass.ds(j * 3 + k, 1), j * 3 + (k + 1), j * 3 + (k - 2))
            hidden((TILES - 2) % 3, TILES - 1, TILES - 2)
            turn_tile((TILES - 1) % 3, 16 * (TILES // 3))
            output((TILES - 3) % 3, slice(TILES - 3, TILES - 2), TILES - 2, TILES - 5)
            hidden((TILES - 1) % 3, TILES, TILES - 1)
            output((TILES - 2) % 3, slice(TILES - 2, TILES - 1), TILES - 1, TILES - 4)
            output((TILES - 1) % 3, slice(TILES - 1, TILES), TILES, TILES - 3)

        @block.vector
        def _(dve):
            def chained(counter, op, value):
                op.then_inc(counter, 1)
                dve.wait_ge(counter, value)

            dve.wait_ge(d_trig, 48)
            nc.vector.tensor_copy(amp_b, amp_s[:, 0:1].broadcast_to((P, BATCHES))).then_inc(s_chain, 1)
            chained(s_chain, nc.vector.tensor_scalar(ang, delta_s[:, :], freq_s[:, 0:1], None, ALU.mult), 2)
            chained(s_chain, nc.vector.tensor_scalar(turns, ang, 1.0 / (2 * 3.141592653589793), ROUND,
                                                     ALU.mult, ALU.add), 3)
            chained(s_chain, nc.vector.tensor_scalar(turns, turns, ROUND, None, ALU.subtract), 4)
            chained(s_chain, nc.vector.scalar_tensor_tensor(out=red, in0=turns, scalar=-TWO_PI_A, in1=ang,
                                                            op0=ALU.mult, op1=ALU.add), 5)
            chained(s_chain, nc.vector.scalar_tensor_tensor(out=ang, in0=turns, scalar=-TWO_PI_B, in1=red,
                                                            op0=ALU.mult, op1=ALU.add), 6)
            nc.vector.scalar_tensor_tensor(out=red, in0=turns, scalar=-TWO_PI_C, in1=ang,
                                           op0=ALU.mult, op1=ALU.add).then_inc(s_red, 1)
            dve.wait_ge(s_red, 1)
            nc.vector.tensor_scalar(red, red, -PI_DOWN, PI_DOWN, ALU.max, ALU.min).then_inc(s_red, 1)
            dve.wait_ge(s_red, 2)
            nc.vector.tensor_scalar(turns, red, -1.0, None, ALU.mult).then_inc(s_red, 1)
            dve.wait_ge(s_red, 3)
            nc.vector.tensor_tensor(ang, red, turns, ALU.max).then_inc(s_red, 1)
            dve.wait_ge(s_red, 4)
            nc.vector.tensor_scalar(cosr, ang, -1.0, 1.5707963267948966, ALU.mult, ALU.add).then_inc(s_chain, 1)
            dve.wait_ge(s_amp, 1)
            dve.wait_ge(s_sin, 2)
            nc.vector.tensor_tensor(cs[:, 0, :], cos_t, amp_t, ALU.mult).then_inc(s_chain, 1)
            nc.vector.tensor_tensor(cs[:, 1, :], sin_t, amp_t, ALU.mult).then_inc(s_chain, 1)
            dve.wait_ge(s_t1, 1)
            nc.vector.tensor_copy(t1[:, :], ps_u[:, 0:P]).then_inc(s_t1c, 1)
            dve.wait_ge(s_wp, 1)
            nc.vector.tensor_copy(wp[:, :], ps_h[:, 0:P]).then_inc(s_wpc, 1)
            nc.vector.memset(seen[:, 0, :], 0.0).then_inc(s_seen, 1)
            dve.wait_ge(s_chain, 9)

            def build_rot(g):
                dve.wait_ge(s_rotc, g + 1)
                if g >= 2:
                    dve.wait_ge(s_h, g - 1)
                for i in range(GB):
                    b = g * GB + i
                    op = nc.vector.scalar_tensor_tensor(out=rot[:, g % 2, i, :], in0=swap[:, :],
                                                        scalar=cs[:, 1, b:b + 1], in1=rot_c[:, g % 2, i, :],
                                                        op0=ALU.mult, op1=ALU.add)
                op.then_inc(s_rot, 1)

            def add_y(g):
                dve.wait_ge(s_y, g + 1)
                if g >= 2:
                    dve.wait_ge(s_yr, g - 1)
                for b in range(g * GB, g * GB + GB):
                    op = nc.vector.scalar_tensor_tensor(out=yT[:, g % 2, cols(b)], in0=ps_y[:, cols(b)],
                                                        scalar=cond_s[:, b, 2 * P + 1:2 * P + 2],
                                                        in1=x1T[:, g, cols(b)], op0=ALU.add, op1=ALU.add)
                op.then_inc(s_yc, 1)

            def moments(g):
                dve.wait_ge(s_yr, g + 1)
                for i in range(GB):
                    op = nc.vector.bn_stats(stats[:, g % 2, i, :], ps_yr[:, i * P:(i + 1) * P])
                op.then_inc(s_stats, 1)
                dve.wait_ge(s_stats, g + 1)
                for i in range(GB):
                    op = nc.vector.bn_aggr(mv[:, g % 2, i, :], stats[:, g % 2, i, :])
                op.then_inc(s_mv, 1)

            def normalise(g):
                dve.wait_ge(s_rstd, g + 1)
                dve.wait_ge(s_mv, g + 1)
                if g >= 2:
                    dve.wait_ge(s_nT, g - 1)
                for i in range(GB):
                    op = nc.vector.tensor_scalar(yhat[:, g % 2, i * P:(i + 1) * P], ps_yr[:, i * P:(i + 1) * P],
                                                 mv[:, g % 2, i, 0:1], rstd[:, g % 2, i:i + 1],
                                                 ALU.subtract, ALU.mult)
                op.then_inc(s_yhat, 1)

            routed = [0]

            def pick(g):
                def then(op):
                    routed[0] += 1
                    chained(s_route, op, routed[0])

                def wide(t):
                    return t.unsqueeze(2).broadcast_to((P, GB, EXPERTS))

                dve.wait_ge(s_log, g + 1)
                if g >= 2:
                    dve.wait_ge(s_pre, g - 1)
                then(nc.vector.tensor_tensor(logits[:, :, :], ps_log.rearrange("p (b e) -> p b e", b=GB),
                                             br_s[:, :].unsqueeze(1).broadcast_to((P, GB, EXPERTS)),
                                             ALU.add))
                then(nc.vector.tensor_reduce(top[:, :], logits[:, :, :], AX.X, ALU.max))
                then(nc.vector.tensor_tensor(tied[:, :, :], logits[:, :, :], wide(top[:, :]), ALU.is_equal))
                then(nc.vector.tensor_tensor(tied[:, :, :], tied[:, :, :], falling[:, :, :], ALU.mult))
                then(nc.vector.tensor_reduce(first[:, :], tied[:, :, :], AX.X, ALU.max))
                nc.vector.tensor_tensor(onehot[:, g % 2, :, :], falling[:, :, :], wide(first[:, :]),
                                        ALU.is_equal).then_inc(s_onehot, 1)
                dve.wait_ge(s_onehot, g + 1)
                then(nc.vector.tensor_reduce(groupsum[:, :], onehot[:, g % 2, :, :].rearrange("p b e -> p e b"),
                                             AX.X, ALU.add))
                nc.vector.tensor_tensor(seen[:, (g + 1) % 2, :], seen[:, g % 2, :], groupsum[:, :], ALU.add)\
                    .then_inc(s_seen, 1)

            def find_slot(g):
                def then(op):
                    routed[0] += 1
                    chained(s_route, op, routed[0])

                dve.wait_ge(s_pre, g + 1)
                then(nc.vector.tensor_tensor(place[:, :, :], ps_pre.rearrange("p (b e) -> p b e", b=GB),
                                             area[:, :].unsqueeze(1).broadcast_to((P, GB, EXPERTS)),
                                             ALU.add))
                then(nc.vector.tensor_tensor(place[:, :, :], place[:, :, :], onehot[:, g % 2, :, :], ALU.mult))
                with nc.allow_low_precision(reason="row numbers are integers below 2**24"):
                    nc.vector.tensor_reduce(slot[:, g * GB:(g + 1) * GB], place[:, :, :], AX.X, ALU.add)\
                        .then_inc(s_slot, 1)

            for stage_name, g in in_turn({"moments": 3, "pick": 5, "y": 2, "slot": 5, "rot": -1, "normalise": 3}):
                if stage_name == "rot" and g == 0:
                    dve.wait_ge(s_const, 9)
                if stage_name == "y":
                    dve.wait_ge(d_cond[g], 16 * GB)
                if stage_name == "pick" and g == 0:
                    dve.wait_ge(s_const, N_CONST)
                    dve.wait_ge(d_small, 64)
                {"rot": build_rot, "y": add_y, "moments": moments, "normalise": normalise, "pick": pick,
                 "slot": find_slot}[stage_name](g)

            tabled = [0]

            def table(op):
                tabled[0] += 1
                chained(s_table, op, tabled[0])

            def over_tiles(v):
                return v.unsqueeze(1).broadcast_to((1, TILES, EXPERTS))

            dve.wait_ge(s_cnt, 1)
            nc.vector.tensor_tensor(pad_row[:, :], ps_cnt[0:1, :], area[0:1, :], ALU.add).then_inc(s_padrow, 1)
            table(nc.vector.tensor_scalar(cnt_i[:, :], ps_cnt[0:1, :], float(P - 1), None, ALU.add))
            table(nc.vector.tensor_scalar(nt_i[:, :], cnt_i[:, :], 7, None, ALU.logical_shift_right))
            table(nc.vector.tensor_copy(nt[:, :], nt_i[:, :]))
            table(nc.vector.tensor_tensor_scan(cum[:, :], ones_8[:, :], nt[:, :], 0.0, ALU.mult, ALU.add))
            table(nc.vector.tensor_scalar(step[:, :], nt[:, :], -float(P), float(PITCH), ALU.mult, ALU.add))
            table(nc.vector.tensor_tensor(past[:, :, :], over_tiles(cum[:, :]),
                                          tau[:, :].unsqueeze(2).broadcast_to((1, TILES, EXPERTS)),
                                          ALU.is_le))
            table(nc.vector.tensor_reduce(tsum[:, :], past[:, :, :], AX.X, ALU.add))
            table(nc.vector.tensor_scalar(tile_e[:, :], tsum[:, :], float(EXPERTS - 1), None, ALU.min))
            table(nc.vector.tensor_tensor(pastw[:, :, :], past[:, :, :], over_tiles(step[:, :]), ALU.mult))
            table(nc.vector.tensor_reduce(tsum[:, :], pastw[:, :, :], AX.X, ALU.add))
            table(nc.vector.tensor_tensor(tsum[:, :], tsum[:, :], tau128[:, :], ALU.add))
            nc.vector.tensor_scalar(tile_r[:, :], tsum[:, :], float(DUMMY), None, ALU.min).then_inc(s_tiles, 1)
            dve.wait_ge(s_tiles, 1)
            dve.wait_ge(d_experts, 32)

            def stage_w1(k, e_at):
                e = dve.value_load(tile_e[0:1, e_at], min_val=0, max_val=EXPERTS - 1)
                return nc.vector.tensor_scalar(stage[:, k, :], w1_s[:, bass.ds(e, 1), :]
                                               .rearrange("p a f -> p (a f)"), 1.0, None, ALU.mult)

            def relu_hi(k, tiles_done):
                dve.wait_ge(s_hhi, tiles_done)
                for c in range(CHUNKS // 2, CHUNKS):
                    op = nc.vector.tensor_scalar(hT[:, k, c * P:(c + 1) * P], ps_hi[:, c * P:(c + 1) * P],
                                                 stage[:, k, FF + c:FF + c + 1], 0.0, ALU.add, ALU.max)
                op.then_inc(s_hhic, 1)

            def result(k, tiles_done, stored=None):
                dve.wait_ge(s_out, tiles_done)
                dve.wait_ge(s_taken, tiles_done)
                if stored is not None:
                    dve.wait_ge(d_res[k], stored)
                nc.vector.tensor_tensor(res[:, k, :], ps_out[k][:, 0:P], resid[:, k, :], ALU.add)\
                    .then_inc(s_res, 1)

            for t in range(3):
                stage_w1(t, slice(t, t + 1)).then_inc(s_stage, 1)
            for t in range(3):
                relu_hi(t, t + 1)
                dve.wait_ge(s_hloc, t + 1)
                dve.wait_ge(s_hhic, t + 1)
                stage_w1(t, slice(t + 3, t + 4)).then_inc(s_stage, 1)
                if t >= 1:
                    result(t - 1, t)
            relu_hi(0, 4)
            dve.wait_ge(s_hloc, 4)
            dve.wait_ge(s_hhic, 4)
            stage_w1(0, slice(6, 7)).then_inc(s_stage, 1)
            result(2, 3)
            with dve.Fori(1, TILES // 3 - 2) as j:
                for k in range(3):
                    t1_ = j * 3 + (k + 2)
                    relu_hi((k + 1) % 3, t1_)
                    dve.wait_ge(s_hloc, t1_)
                    dve.wait_ge(s_hhic, t1_)
                    stage_w1((k + 1) % 3, bass.ds(j * 3 + (k + 4), 1)).then_inc(s_stage, 1)
                    result(k, j * 3 + (k + 1), j * 16)
            for t in range(TILES - 5, TILES):
                relu_hi(t % 3, t + 1)
                if t + 3 < TILES:
                    dve.wait_ge(s_hloc, t + 1)
                    dve.wait_ge(s_hhic, t + 1)
                    stage_w1(t % 3, slice(t + 3, t + 4)).then_inc(s_stage, 1)
                result((t - 1) % 3, t, 16 * ((t - 1) // 3))
            result((TILES - 1) % 3, TILES, 16 * ((TILES - 1) // 3))


def kernel(**inputs):
    import numpy as np
    import concourse.bacc as _bacc
    from concourse import mybir as _mybir
    from concourse.bass_utils import run_bass_kernel_spmd as _run

    a = {k: np.asarray(v) for k, v in inputs.items()}
    laid = {
        "xT": a["x"].transpose(2, 0, 1).reshape(P, TOKENS),
        "w0": np.stack([a["L0_ffn_weight"].T, a["L0_ffn_aux_weight1"].T, a["L0_ffn_aux_weight2"]], axis=1),
        "bias0": a["L0_ffn_bias"],
        "amp": np.repeat(a["L0_cond_amplitudes"], 2),
        "freq": np.repeat(a["L0_cond_frequencies"], 2),
        "delta": a["condB_deltat"],
        "prof": a["itok_B_0_6"],
        "cond": np.concatenate([a["L1_cond_down_w"], a["L1_cond_up_w"], a["L1_cond_down_b"][:, :, None],
                                a["L1_cond_up_b"][:, :, None], a["L1_cond_ln_g"][:, :, None],
                                a["L1_cond_ln_b"][:, :, None]], axis=2),
        "wr": a["L1_ffn_Wr"].T,
        "br": a["L1_ffn_br"],
        "w1": np.concatenate([a["L1_ffn_W1"].transpose(2, 0, 1),
                              a["L1_ffn_b1"].reshape(EXPERTS, CHUNKS, P).transpose(2, 0, 1)], axis=2),
        "w2": a["L1_ffn_W2"].reshape(EXPERTS, P, CHUNKS, P).transpose(3, 0, 2, 1),
        "b2": a["L1_ffn_b2"],
    }
    nc = _bacc.Bacc("TRN2", target_bir_lowering=False, num_devices=1)
    arrays, args = {}, []
    for name, v in laid.items():
        v = np.ascontiguousarray(v)
        arrays[f"in_{name}"] = v
        args.append(nc.dram_tensor(f"in_{name}", v.shape, _mybir.dt.from_np(v.dtype), kind="ExternalInput").ap())
    args.append(nc.dram_tensor("out_0", (BATCHES, P, P), _mybir.dt.float32, kind="ExternalOutput").ap())
    adaln_moe(nc, *args)
    r = _run(nc, [arrays], core_ids=[0])
    return r.results[0]["out_0"]
```

```python
from contextlib import ExitStack

import concourse.bass as bass
from concourse import mybir

P = 128
BATCHES = 32
TOKENS = BATCHES * P
EXPERTS = 8
PROFILES = 8
FF = 512
CHUNKS = FF // P
GB = 4
GROUPS = BATCHES // GB
GN = GB * P
PITCH = TOKENS + P
DUMMY = EXPERTS * PITCH
TILES = TOKENS // P + EXPERTS - 1
SOONER = 6
SOON = SOONER * GB - EXPERTS + 1
LATER = TILES - SOON
ROW = 260
ID = 2 * P
NO_TOKEN = float(1 << 20)
CW = 260
EB = FF + CHUNKS
EW = EB + P
EPS = 1e-5

F32 = mybir.dt.float32
I32 = mybir.dt.int32
BF16 = mybir.dt.bfloat16
ALU = mybir.AluOpType
ACT = mybir.ActivationFunctionType
AX = mybir.AxisListType

TWO_PI_A, TWO_PI_B, TWO_PI_C = 6.28125, 0.0019340515136718750, 1.2556659146e-06
PI_DOWN = 3.1415925
SP, PE, DVE = mybir.EngineType.SP, mybir.EngineType.PE, mybir.EngineType.DVE
ROUND = 1.5 * 2.0 ** 23


def adaln_moe(nc, xT, w0, bias0, amp, freq, delta, prof, cond, wr, br, w1, w2, b2, out):
    rows_d = nc.dram_tensor("expert_rows", (DUMMY + P, ROW), F32).ap()
    out_rows = out.rearrange("b s d -> (b s) d")

    with ExitStack() as ctx:
        def sb(name, shape, dt=F32):
            return ctx.enter_context(nc.sbuf_tensor(name, shape, dt))

        def sem(name):
            return ctx.enter_context(nc.semaphore(name))

        w0_s = sb("w0_s", [P, 3, P])
        t1 = sb("t1", [P, P])
        wp = sb("wp", [P, P])
        bias0_s = sb("bias0_s", [P, 1])
        prof_s = sb("prof_s", [1, BATCHES], I32)
        amp_s = sb("amp_s", [P, 1])
        freq_s = sb("freq_s", [P, 1])
        delta_s = sb("delta_s", [P, BATCHES])
        cond_s = sb("cond_s", [P, BATCHES, CW])
        wr_s = sb("wr_s", [P, EXPERTS])
        br_s = sb("br_s", [P, EXPERTS])
        w1_s = sb("w1_s", [P, EXPERTS, EW])
        w2_s = sb("w2_s", [P, EXPERTS, CHUNKS, P])

        ident = sb("ident", [P, P])
        swap = sb("swap", [P, P])
        before = sb("before", [P, P], BF16)
        ones_b = sb("ones_b", [P, P], BF16)
        ones_8 = sb("ones_8", [1, EXPERTS])
        neg_half = sb("neg_half", [P, GB])
        falling = sb("falling", [P, GB, EXPERTS])
        area = sb("area", [P, EXPERTS])
        tau = sb("tau", [1, TILES])
        tau128 = sb("tau128", [1, TILES])
        pad = sb("pad", [P, ROW])

        trig = sb("trig", [P, 8, BATCHES])
        ang, turns, red, cosr, sin_t, cos_t, amp_t, amp_b = (trig[:, i, :] for i in range(8))
        cs = sb("cs", [P, 2, BATCHES])
        rot_c = sb("rot_c", [P, 2, GB, P])
        rot = sb("rot", [P, 2, GB, P])

        x1T = sb("x1T", [P, GROUPS, GN])
        u = sb("u", [P, 2, GN])
        tanh_s = sb("tanh_s", [P, 2, GN])
        zT = sb("zT", [P, 2, GN])
        yT = sb("yT", [P, 2, GN])
        yhat = sb("yhat", [P, 2, GN])
        xnT = sb("xnT", [P, 2, GN])
        stats = sb("stats", [P, 2, GB, 6])
        mv = sb("mv", [P, 2, GB, 2])
        vareps = sb("vareps", [P, 2, GB])
        rstd = sb("rstd", [P, 2, GB])
        payload = sb("payload", [P, BATCHES, ROW])

        logits = sb("logits", [P, GB, EXPERTS])
        top = sb("top", [P, GB])
        tied = sb("tied", [P, GB, EXPERTS])
        first = sb("first", [P, GB])
        onehot = sb("onehot", [P, 2, GB, EXPERTS], BF16)
        seen = sb("seen", [P, 2, EXPERTS], BF16)
        groupsum = sb("groupsum", [P, EXPERTS])
        place = sb("place", [P, GB, EXPERTS])
        slot = sb("slot", [P, BATCHES], I32)

        cnt_i = sb("cnt_i", [1, EXPERTS], I32)
        nt_i = sb("nt_i", [1, EXPERTS], I32)
        nt = sb("nt", [1, EXPERTS])
        capped = sb("capped", [1, 1 + EXPERTS])
        taken = sb("taken", [1, EXPERTS + 1])
        step_up = sb("step_up", [1, EXPERTS])
        taken_0 = sb("taken_0", [1, 1])
        cum = sb("cum", [1, EXPERTS])
        jump = sb("jump", [1, EXPERTS])
        past = sb("past", [1, TILES, EXPERTS])
        pastw = sb("pastw", [1, TILES, EXPERTS])
        tsum = sb("tsum", [1, TILES])
        pad_row = sb("pad_row", [1, EXPERTS], I32)
        tile_e = sb("tile_e", [1, TILES], I32)
        tile_r = sb("tile_r", [1, TILES], I32)

        rows = sb("rows", [P, 3, ROW])
        ids = sb("ids", [P, 6], I32)
        zero_i = sb("zero_i", [P, 1], I32)
        tileT = sb("tileT", [P, 3, P])
        stage = sb("stage", [P, 3, EW])
        hT = sb("hT", [P, 3, FF])
        resid = sb("resid", [P, 3, P])
        res = sb("res", [P, 3, P])

        bank = [ctx.enter_context(nc.psum_tensor(f"bank{i}", [P, GN], F32)) for i in range(8)]
        ps_u, ps_h, ps_z, ps_y, ps_yr, ps_nT, ps_nr, ps_r = bank
        ps_x1 = ps_u
        ps_log = ps_r[:, 0:GB * EXPERTS]
        ps_pre = ps_r[:, 64:64 + GB * EXPERTS]
        ps_cnt = ps_r[:, 128:128 + EXPERTS]
        ps_t = bank[2]
        ps_lo, ps_hi = bank[0], bank[1]
        ps_out = bank[3:6]

        d_w0 = sem("d_w0")
        d_trig = sem("d_trig")
        d_prof = sem("d_prof")
        d_small = sem("d_small")
        d_x = [sem(f"d_x{g}") for g in range(GROUPS)]
        d_cond = [sem(f"d_cond{g}") for g in range(GROUPS)]
        d_experts = sem("d_experts")
        d_scatter = sem("d_scatter")
        d_late = sem("d_late")
        d_pads = sem("d_pads")
        d_dummy = sem("d_dummy")
        d_rows = [sem(f"d_rows{k}") for k in range(3)]
        d_res = [sem(f"d_res{k}") for k in range(3)]

        s_const = sem("s_const")
        s_t1 = sem("s_t1")
        s_t1c = sem("s_t1c")
        s_wp = sem("s_wp")
        s_wpc = sem("s_wpc")
        s_chain = sem("s_chain")
        s_red = sem("s_red")
        s_amp = sem("s_amp")
        s_sin = sem("s_sin")
        s_rotc = sem("s_rotc")
        s_rot = sem("s_rot")
        s_u = sem("s_u")
        s_uc = sem("s_uc")
        s_h = sem("s_h")
        s_tanh = sem("s_tanh")
        s_x1T = sem("s_x1T")
        s_x1 = sem("s_x1")
        s_x1c = sem("s_x1c")
        s_z = sem("s_z")
        s_zc = sem("s_zc")
        s_y = sem("s_y")
        s_yc = sem("s_yc")
        s_yr = sem("s_yr")
        s_stats = sem("s_stats")
        s_mv = sem("s_mv")
        s_var = sem("s_var")
        s_rstd = sem("s_rstd")
        s_yhat = sem("s_yhat")
        s_nT = sem("s_nT")
        s_nTc = sem("s_nTc")
        s_nr = sem("s_nr")
        s_nrc = sem("s_nrc")
        s_log = sem("s_log")
        s_route = sem("s_route")
        s_onehot = sem("s_onehot")
        s_seen = sem("s_seen")
        s_pre = sem("s_pre")
        s_slot = sem("s_slot")
        s_counted = sem("s_counted")
        s_padrow = sem("s_padrow")
        s_table = sem("s_table")
        s_tiles = sem("s_tiles")
        s_tT = sem("s_tT")
        s_tTc = sem("s_tTc")
        s_stage = sem("s_stage")
        s_hlo = sem("s_hlo")
        s_hhi = sem("s_hhi")
        s_hloc = sem("s_hloc")
        s_hhic = sem("s_hhic")
        s_out = sem("s_out")
        s_res = sem("s_res")
        s_taken = sem("s_taken")
        s_resid = sem("s_resid")

        N_CONST = 18
        N_ALL = N_CONST + 1
        block = ctx.enter_context(nc.Block())

        def loaded(engine, table, first, high, n=3):
            at = slice(first, first + n) if isinstance(first, int) else bass.ds(first, n)
            return nc.values_load_multi_w_load_instructions(
                table[0:1, at], engines=(engine,), min_val=0, max_val=high,
                skip_runtime_bounds_check_because="the table's values are in this range as they are made")[1]

        def cols(b):
            return slice(b % GB * P, b % GB * P + P)

        def in_turn(lags):
            for t in range(min(lags.values()), GROUPS + max(lags.values())):
                for stage_name, lag in lags.items():
                    if 0 <= t - lag < GROUPS:
                        yield stage_name, t - lag

        @block.sync
        def _(sp):
            sp.dma_start(delta_s[:, :], delta.partition_broadcast(P)).then_inc(d_trig, 16)
            sp.dma_start(freq_s[:, :], freq.rearrange("(p a) -> p a", a=1)).then_inc(d_trig, 16)
            sp.dma_start(amp_s[:, :], amp.rearrange("(p a) -> p a", a=1)).then_inc(d_trig, 16)
            sp.dma_start(x1T[:, 0, :], xT[:, 0:GN]).then_inc(d_x[0], 16)
            sp.dma_start(prof_s[:, :], prof.rearrange("(a n) -> a n", a=1)).then_inc(d_prof, 16)
            sp.dma_start(x1T[:, 1, :], xT[:, GN:2 * GN]).then_inc(d_x[1], 16)
            sp.wait_ge(d_prof, 16)
            for g in range(GROUPS):
                for b in range(g * GB, g * GB + GB):
                    p = sp.value_load(prof_s[0:1, b:b + 1], min_val=0, max_val=PROFILES - 1)
                    sp.dma_start(cond_s[:, b, :], cond[bass.ds(p, 1), :, :].rearrange("a p c -> (a p) c"))\
                        .then_inc(d_cond[g], 16)
                if g + 2 < GROUPS:
                    sp.dma_start(x1T[:, g + 2, :], xT[:, (g + 2) * GN:(g + 3) * GN]).then_inc(d_x[g + 2], 16)
            sp.dma_start(w1_s[:, :, 0:EB], w1).then_inc(d_experts, 16)
            sp.dma_start(w1_s[:, :, EB:EW], b2.partition_broadcast(P)).then_inc(d_experts, 16)
            sp.dma_start(w2_s[:, :, :, :], w2).then_inc(d_experts, 16)

            def load_rows(k, r):
                sp.dma_start(rows[:, k, :], rows_d[bass.ds(r, P), :]).then_inc(d_rows[k], 16)

            sp.wait_ge(s_tiles, 1)
            starts = loaded(SP, tile_r, 0, DUMMY)
            sp.wait_ge(d_scatter, 16 * SOONER * GB)
            for t in range(3):
                load_rows(t, starts[t])

            def slot_free(tiles_done):
                sp.wait_ge(s_tT, tiles_done)
                sp.wait_ge(s_taken, tiles_done)
                sp.wait_ge(s_resid, tiles_done)

            starts = loaded(SP, tile_r, 3, DUMMY)
            ends = None
            for k in range(3):
                slot_free(k + 1)
                load_rows(k, starts[k])
                if ends is None:
                    sp.wait_ge(s_padrow, 1)
                    ends = loaded(SP, pad_row, 0, DUMMY - P, EXPERTS)
                for e in range(k * 3, min(k * 3 + 3, EXPERTS)):
                    sp.dma_start(rows_d[bass.ds(ends[e], P), :], pad[:, :]).then_inc(d_pads, 16)

            def load_more(first, last):
                with sp.Fori(first, last) as j:
                    starts = loaded(SP, tile_r, j * 3 + 3, DUMMY)
                    for k in range(3):
                        slot_free(j * 3 + (k + 1))
                        load_rows(k, starts[k])

            load_more(1, SOON // 3 - 1)
            sp.wait_ge(s_tiles, 2)
            sp.wait_ge(d_late, 16 * (BATCHES - SOONER * GB))
            sp.wait_ge(d_pads, 16 * EXPERTS)
            sp.wait_ge(d_dummy, 16)
            load_more(SOON // 3 - 1, TILES // 3 - 1)

        @block.gpsimd
        def _(pool):
            pool.memset(ident[:, :], 0.0).then_inc(s_const, 1)
            pool.memset(swap[:, :], 0.0).then_inc(s_const, 1)
            pool.memset(pad[:, :], 0.0).then_inc(s_const, 1)
            pool.memset(before[:, :], 1.0).then_inc(s_const, 1)
            pool.memset(ones_b[:, :], 1.0).then_inc(s_const, 1)
            pool.memset(neg_half[:, :], -0.5).then_inc(s_const, 1)
            pool.wait_ge(s_const, 6)
            pool.affine_select(out=ident[:, :], in_=ident[:, :], compare_op=ALU.not_equal, fill=1.0, base=0,
                               pattern=[[-1, P]], channel_multiplier=1).then_inc(s_const, 1)
            pairs = swap[:, :].rearrange("p (f two) -> p f two", two=2)
            pool.affine_select(out=pairs[:, :, 0], in_=pairs[:, :, 0], compare_op=ALU.not_equal, fill=-1.0,
                               base=-1, pattern=[[-2, P // 2]], channel_multiplier=1).then_inc(s_const, 1)
            pool.affine_select(out=pairs[:, :, 1], in_=pairs[:, :, 1], compare_op=ALU.not_equal, fill=1.0,
                               base=0, pattern=[[-2, P // 2]], channel_multiplier=1).then_inc(s_const, 1)
            pool.wait_ge(d_trig, 48)
            pool.wait_ge(s_chain, 1)
            pool.tensor_tensor(amp_t[:, 0:GB], amp_b[:, 0:GB], delta_s[:, 0:GB], ALU.pow).then_inc(s_amp, 1)

            def cos_part(g):
                pool.wait_ge(s_chain, 9 if g == 0 else 11)
                if g >= 2:
                    pool.wait_ge(s_rot, g - 1)
                for i in range(GB):
                    b = g * GB + i
                    op = pool.tensor_scalar(rot_c[:, g % 2, i, :], ident[:, :], cs[:, 0, b:b + 1], None, ALU.mult)
                op.then_inc(s_rotc, 1)

            cos_part(0)
            pool.tensor_tensor(amp_t[:, GB:], amp_b[:, GB:], delta_s[:, GB:], ALU.pow).then_inc(s_amp, 1)
            pool.affine_select(out=before[:, :], in_=before[:, :], compare_op=ALU.is_gt, fill=0.0, base=0,
                               pattern=[[1, P]], channel_multiplier=-1).then_inc(s_const, 1)
            pool.memset(pad[:, ID:ID + 1].bitcast(I32), int(NO_TOKEN)).then_inc(s_const, 1)
            pool.iota(falling[:, :, :], pattern=[[0, GB], [-1, EXPERTS]], base=EXPERTS, channel_multiplier=0,
                      allow_small_or_imprecise_dtypes=True).then_inc(s_const, 1)
            pool.iota(area[:, :], pattern=[[PITCH, EXPERTS]], base=0, channel_multiplier=0,
                      allow_small_or_imprecise_dtypes=True).then_inc(s_const, 1)
            pool.iota(tau[:, :], pattern=[[1, TILES]], base=0, channel_multiplier=0,
                      allow_small_or_imprecise_dtypes=True).then_inc(s_const, 1)
            pool.iota(tau128[:, :], pattern=[[P, TILES]], base=0, channel_multiplier=0,
                      allow_small_or_imprecise_dtypes=True).then_inc(s_const, 1)
            pool.memset(payload[:, :, ID:ROW], 0.0).then_inc(s_const, 1)
            pool.memset(ones_8[:, :], 1.0).then_inc(s_const, 1)
            pool.memset(zero_i[:, :], 0).then_inc(s_const, 1)
            pool.wait_ge(s_const, N_CONST)
            pool.iota(payload[:, :, ID].bitcast(I32), pattern=[[P, BATCHES]], base=0, channel_multiplier=1)\
                .then_inc(s_const, 1)
            pool.dma_start(rows_d[DUMMY:DUMMY + P, :], pad[:, :]).then_inc(d_dummy, 16)

            def add_x(g):
                pool.wait_ge(s_tanh, g + 1)
                pool.wait_ge(s_u, g + 1)
                pool.tensor_tensor(x1T[:, g, :], x1T[:, g, :], tanh_s[:, g % 2, :], ALU.add).then_inc(s_x1T, 1)

            def deviation(g):
                pool.wait_ge(s_mv, g + 1)
                pool.tensor_scalar(vareps[:, g % 2, :], mv[:, g % 2, :, 1], EPS, None, ALU.add).then_inc(s_var, 1)
                pool.wait_ge(s_var, g + 1)
                pool.tensor_tensor(rstd[:, g % 2, :], vareps[:, g % 2, :], neg_half[:, :], ALU.pow)\
                    .then_inc(s_rstd, 1)

            def scatter(g):
                pool.wait_ge(s_slot, g + 1)
                pool.wait_ge(s_nrc, g + 1)
                pool.wait_ge(s_x1c, g + 1)
                pool.wait_ge(s_const, N_ALL)
                for b in range(g * GB, g * GB + GB):
                    pool.indirect_dma_start(
                        out=rows_d, out_offset=bass.IndirectOffsetOnAxis(ap=slot[:, b:b + 1], axis=0),
                        in_=payload[:, b, :], in_offset=None)\
                        .then_inc(d_scatter if g < SOONER else d_late, 16)

            last_token = pool.to_reg(TOKENS - 1)

            def take_ids(k, i, arrivals):
                pool.wait_ge(d_rows[k], arrivals)
                pool.tensor_tensor(ids[:, i:i + 1], rows[:, k, ID:ID + 1].bitcast(I32), zero_i[:, :], ALU.add)\
                    .then_inc(s_taken, 1)

            def store(k, i):
                pool.indirect_dma_start(
                    out=out_rows, out_offset=bass.IndirectOffsetOnAxis(ap=ids[:, i:i + 1], axis=0),
                    in_=res[:, k, :], in_offset=None, bounds_check=last_token, oob_is_err=False)\
                    .then_inc(d_res[k], 16)

            for stage_name, g in in_turn({"cos": -2, "dev": 3, "add": 0, "scatter": 5}):
                if (stage_name, g) == ("scatter", GROUPS - 1):
                    for t in range(3):
                        take_ids(t, t, 16)
                if (stage_name, g) != ("cos", 0):
                    {"cos": cos_part, "add": add_x, "dev": deviation, "scatter": scatter}[stage_name](g)
            pool.wait_ge(s_res, 1)
            pool.wait_ge(s_taken, 1)
            store(0, 0)
            with pool.Fori(0, (TILES - 3) // 6) as j:
                for q in range(6):
                    pool.wait_ge(s_res, j * 6 + (q + 2))
                    pool.wait_ge(s_taken, j * 6 + (q + 3))
                    take_ids(q % 3, (q + 3) % 6, j * 32 + 16 * (q // 3 + 2))
                    store((q + 1) % 3, (q + 1) % 6)
            for t in range(TILES - 2, TILES):
                pool.wait_ge(s_res, t + 1)
                pool.wait_ge(s_taken, t + 1)
                store(t % 3, t % 6)
            for k in range(3):
                pool.wait_ge(d_res[k], 16 * (TILES // 3))

        @block.scalar
        def _(act):
            act.dma_start(w0_s[:, :, :], w0).then_inc(d_w0, 16)
            act.dma_start(bias0_s[:, :], bias0.rearrange("(p a) -> p a", a=1)).then_inc(d_small, 16)
            act.dma_start(wr_s[:, :], wr).then_inc(d_small, 16)
            act.dma_start(br_s[:, :], br.partition_broadcast(P)).then_inc(d_small, 16)
            act.wait_ge(s_chain, 7)
            nc.scalar.activation(sin_t, red, ACT.Sin).then_inc(s_sin, 1)
            nc.scalar.activation(cos_t, cosr, ACT.Sin).then_inc(s_sin, 1)

            def copy_u(g):
                act.wait_ge(s_u, g + 1)
                if g >= 2:
                    act.wait_ge(s_h, g - 1)
                nc.scalar.activation(u[:, g % 2, :], ps_u[:, :], ACT.Copy).then_inc(s_uc, 1)

            def tanh(g):
                act.wait_ge(s_h, g + 1)
                if g >= 2:
                    act.wait_ge(s_x1T, g - 1)
                nc.scalar.activation(tanh_s[:, g % 2, :], ps_h[:, :], ACT.Tanh, bias=bias0_s[:, 0:1])\
                    .then_inc(s_tanh, 1)

            def copy_x1(g):
                act.wait_ge(s_x1, g + 1)
                nc.scalar.activation(payload[:, g * GB:(g + 1) * GB, P:2 * P],
                                     ps_x1[:, :].rearrange("p (b d) -> p b d", b=GB), ACT.Copy).then_inc(s_x1c, 1)

            def relu_z(g):
                act.wait_ge(s_z, g + 1)
                if g >= 2:
                    act.wait_ge(s_y, g - 1)
                for b in range(g * GB, g * GB + GB):
                    op = nc.scalar.activation(zT[:, g % 2, cols(b)], ps_z[:, cols(b)], ACT.Relu,
                                              bias=cond_s[:, b, 2 * P:2 * P + 1])
                op.then_inc(s_zc, 1)

            def gain(g):
                act.wait_ge(s_nT, g + 1)
                if g >= 2:
                    act.wait_ge(s_log, g - 1)
                for b in range(g * GB, g * GB + GB):
                    op = nc.scalar.activation(xnT[:, g % 2, cols(b)], ps_nT[:, cols(b)], ACT.Identity,
                                              scale=cond_s[:, b, 2 * P + 2:2 * P + 3],
                                              bias=cond_s[:, b, 2 * P + 3:2 * P + 4])
                op.then_inc(s_nTc, 1)

            def copy_xn(g):
                act.wait_ge(s_nr, g + 1)
                nc.scalar.activation(payload[:, g * GB:(g + 1) * GB, 0:P],
                                     ps_nr[:, :].rearrange("p (b d) -> p b d", b=GB), ACT.Copy).then_inc(s_nrc, 1)

            act.wait_ge(d_small, 48)
            for stage_name, g in in_turn({"u": 0, "gain": 4, "tanh": 0, "x1": 1, "z": 1, "xn": 4}):
                if stage_name == "z":
                    act.wait_ge(d_cond[g], 16 * GB)
                {"u": copy_u, "tanh": tanh, "x1": copy_x1, "z": relu_z, "gain": gain, "xn": copy_xn}[stage_name](g)

            def copy_tile(k, tiles_done):
                act.wait_ge(s_tT, tiles_done)
                nc.scalar.activation(tileT[:, k, :], ps_t[:, k * P:(k + 1) * P], ACT.Copy).then_inc(s_tTc, 1)

            def relu_lo(k, tiles_done):
                act.wait_ge(s_hlo, tiles_done)
                for c in range(CHUNKS // 2):
                    op = nc.scalar.activation(hT[:, k, c * P:(c + 1) * P], ps_lo[:, c * P:(c + 1) * P],
                                              ACT.Relu, bias=stage[:, k, FF + c:FF + c + 1])
                op.then_inc(s_hloc, 1)

            copy_tile(0, 1)
            relu_lo(0, 1)
            copy_tile(1, 2)
            with act.Fori(0, TILES // 3 - 1) as j:
                for k in range(3):
                    relu_lo((k + 1) % 3, j * 3 + (k + 2))
                    copy_tile((k + 2) % 3, j * 3 + (k + 3))
            relu_lo((TILES - 2) % 3, TILES - 1)
            copy_tile((TILES - 1) % 3, TILES)
            relu_lo((TILES - 1) % 3, TILES)

        @block.tensor
        def _(pe):
            pe.wait_ge(d_w0, 16)
            nc.tensor.matmul(ps_u[:, 0:P], w0_s[:, 1, :], w0_s[:, 2, :], start=True, stop=True).then_inc(s_t1, 1)
            pe.wait_ge(s_t1c, 1)
            nc.tensor.matmul(ps_h[:, 0:P], w0_s[:, 0, :], t1[:, :], start=True, stop=True).then_inc(s_wp, 1)
            pe.wait_ge(s_wpc, 1)
            pe.wait_ge(s_const, 9)

            def mul_w(g):
                pe.wait_ge(d_x[g], 16)
                if g >= 1:
                    pe.wait_ge(s_uc, g)
                if g >= 2:
                    pe.wait_ge(s_x1c, g - 1)
                for i in range(GB):
                    op = nc.tensor.matmul(ps_u[:, i * P:(i + 1) * P], x1T[:, g, i * P:(i + 1) * P], wp[:, :],
                                          start=True, stop=True)
                op.then_inc(s_u, 1)

            def rotate(g):
                pe.wait_ge(s_uc, g + 1)
                pe.wait_ge(s_rot, g + 1)
                if g >= 1:
                    pe.wait_ge(s_tanh, g)
                for i in range(GB):
                    op = nc.tensor.matmul(ps_h[:, i * P:(i + 1) * P], u[:, g % 2, i * P:(i + 1) * P],
                                          rot[:, g % 2, i, :], start=True, stop=True)
                op.then_inc(s_h, 1)

            def turn_x1(g):
                pe.wait_ge(s_x1T, g + 1)
                if g >= 1:
                    pe.wait_ge(s_x1c, g)
                pe.wait_ge(s_uc, min(g + 2, GROUPS))
                for i in range(GB):
                    op = nc.tensor.transpose(ps_x1[:, i * P:(i + 1) * P], x1T[:, g, i * P:(i + 1) * P], ident[:, :])
                op.then_inc(s_x1, 1)

            def down(g):
                pe.wait_ge(d_cond[g], 16 * GB)
                if g >= 1:
                    pe.wait_ge(s_zc, g)
                for b in range(g * GB, g * GB + GB):
                    op = nc.tensor.matmul(ps_z[:, cols(b)], cond_s[:, b, 0:P], x1T[:, g, cols(b)],
                                          start=True, stop=True)
                op.then_inc(s_z, 1)

            def up(g):
                pe.wait_ge(s_zc, g + 1)
                if g >= 1:
                    pe.wait_ge(s_yc, g)
                for b in range(g * GB, g * GB + GB):
                    op = nc.tensor.matmul(ps_y[:, cols(b)], cond_s[:, b, P:2 * P], zT[:, g % 2, cols(b)],
                                          start=True, stop=True)
                op.then_inc(s_y, 1)

            def turn_y(g):
                pe.wait_ge(s_yc, g + 1)
                if g >= 1:
                    pe.wait_ge(s_yhat, g)
                for i in range(GB):
                    op = nc.tensor.transpose(ps_yr[:, i * P:(i + 1) * P], yT[:, g % 2, i * P:(i + 1) * P],
                                             ident[:, :])
                op.then_inc(s_yr, 1)

            def turn_yhat(g):
                pe.wait_ge(s_yhat, g + 1)
                if g >= 1:
                    pe.wait_ge(s_nTc, g)
                for i in range(GB):
                    op = nc.tensor.transpose(ps_nT[:, i * P:(i + 1) * P], yhat[:, g % 2, i * P:(i + 1) * P],
                                             ident[:, :])
                op.then_inc(s_nT, 1)

            def route(g):
                pe.wait_ge(s_nTc, g + 1)
                if g >= 1:
                    pe.wait_ge(s_slot, g)
                    pe.wait_ge(s_nrc, g)
                for i in range(GB):
                    op = nc.tensor.transpose(ps_nr[:, i * P:(i + 1) * P], xnT[:, g % 2, i * P:(i + 1) * P],
                                             ident[:, :])
                op.then_inc(s_nr, 1)
                for i in range(GB):
                    op = nc.tensor.matmul(ps_log[:, i * EXPERTS:(i + 1) * EXPERTS],
                                          xnT[:, g % 2, i * P:(i + 1) * P], wr_s[:, :], start=True, stop=True)
                op.then_inc(s_log, 1)

            def prefix(g):
                pe.wait_ge(s_onehot, g + 1)
                pe.wait_ge(s_const, N_CONST)
                if g >= 1:
                    pe.wait_ge(s_slot, g)
                oh = onehot[:, g % 2, :, :].rearrange("p b e -> p (b e)")
                nc.tensor.matmul(ps_pre, before[:, :], oh, start=True, stop=False, skip_group_check=True)
                for back in range(1, GB):
                    n = (GB - back) * EXPERTS
                    nc.tensor.matmul(ps_pre[:, back * EXPERTS:], ones_b[:, :], oh[:, 0:n], start=False, stop=False,
                                     skip_group_check=True)
                pe.wait_ge(s_seen, g + 1)
                for i in range(GB):
                    op = nc.tensor.matmul(ps_pre[:, i * EXPERTS:(i + 1) * EXPERTS], ones_b[:, :],
                                          seen[:, g % 2, :], start=False, stop=(i == GB - 1),
                                          skip_group_check=True)
                if g in (SOONER - 1, GROUPS - 1):
                    pe.wait_ge(s_seen, g + 2)
                    op = nc.tensor.matmul(ps_cnt, ones_b[:, :], seen[:, (g + 1) % 2, :], start=True, stop=True,
                                          skip_group_check=True)
                op.then_inc(s_pre, 1)

            pe.wait_ge(d_small, 48)
            steps = {"u": mul_w, "up": up, "h": rotate, "prefix": prefix, "yr": turn_y, "x1": turn_x1, "z": down,
                     "nT": turn_yhat, "route": route}
            for stage_name, g in in_turn({"yr": 3, "u": 0, "nT": 4, "up": 2, "prefix": 5, "h": 0, "x1": 1, "z": 1,
                                          "route": 4}):
                if (stage_name, g) != ("prefix", GROUPS - 1):
                    steps[stage_name](g)

            def turn_tile(k, arrivals):
                pe.wait_ge(d_rows[k], arrivals)
                nc.tensor.transpose(ps_t[:, k * P:(k + 1) * P], rows[:, k, 0:P], ident[:, :]).then_inc(s_tT, 1)

            def hidden(k, tiles_ready, read=None):
                pe.wait_ge(s_stage, tiles_ready)
                pe.wait_ge(s_tTc, tiles_ready)
                for half, used, done in ((ps_lo, s_hloc, s_hlo), (ps_hi, s_hhic, s_hhi)):
                    if read is not None:
                        pe.wait_ge(used, read)
                    for c in range(CHUNKS // 2) if half is ps_lo else range(CHUNKS // 2, CHUNKS):
                        op = nc.tensor.matmul(half[:, c * P:(c + 1) * P], stage[:, k, c * P:(c + 1) * P],
                                              tileT[:, k, :], start=True, stop=True)
                    op.then_inc(done, 1)

            def output(k, e, tiles_ready, freed=None):
                pe.wait_ge(s_hloc, tiles_ready)
                pe.wait_ge(s_hhic, tiles_ready)
                if freed is not None:
                    pe.wait_ge(s_res, freed)
                for c in range(CHUNKS):
                    w2_e = w2_s[:, bass.ds(e, 1), c, :].rearrange("p a d -> p (a d)")
                    op = nc.tensor.matmul(ps_out[k][:, 0:P], hT[:, k, c * P:(c + 1) * P], w2_e,
                                          start=(c == 0), stop=(c == CHUNKS - 1))
                op.then_inc(s_out, 1)

            pe.wait_ge(s_tiles, 1)
            pe.wait_ge(s_x1c, GROUPS)
            pe.wait_ge(d_experts, 48)
            turn_tile(0, 16)
            expert = loaded(PE, tile_e, 0, EXPERTS - 1)
            hidden(0, 1)
            prefix(GROUPS - 1)
            turn_tile(1, 16)
            hidden(1, 2, 1)
            turn_tile(2, 16)
            output(0, expert[0], 1)
            hidden(2, 3, 2)
            turn_tile(0, 32)
            output(1, expert[1], 2)
            hidden(0, 4, 3)
            turn_tile(1, 32)
            output(2, expert[2], 3)

            def tiles_between(first, last):
                with pe.Fori(first, last) as j:
                    for k in range(3):
                        hidden((k + 1) % 3, j * 3 + (k + 2), j * 3 + (k + 1))
                        turn_tile((k + 2) % 3, j * 16 + (16 if k == 0 else 32))
                        if k == 0:
                            expert = loaded(PE, tile_e, j * 3, EXPERTS - 1)
                        output(k, expert[k], j * 3 + (k + 1), j * 3 + (k - 2))

            tiles_between(1, SOON // 3)
            pe.wait_ge(s_tiles, 2)
            tiles_between(SOON // 3, TILES // 3 - 1)
            expert = loaded(PE, tile_e, TILES - 3, EXPERTS - 1)
            hidden((TILES - 2) % 3, TILES - 1, TILES - 2)
            turn_tile((TILES - 1) % 3, 16 * (TILES // 3))
            output((TILES - 3) % 3, expert[0], TILES - 2, TILES - 5)
            hidden((TILES - 1) % 3, TILES, TILES - 1)
            output((TILES - 2) % 3, expert[1], TILES - 1, TILES - 4)
            output((TILES - 1) % 3, expert[2], TILES, TILES - 3)

        @block.vector
        def _(dve):
            def chained(counter, op, value):
                op.then_inc(counter, 1)
                dve.wait_ge(counter, value)

            dve.wait_ge(d_trig, 48)
            nc.vector.tensor_copy(amp_b, amp_s[:, 0:1].broadcast_to((P, BATCHES))).then_inc(s_chain, 1)
            chained(s_chain, nc.vector.tensor_scalar(ang, delta_s[:, :], freq_s[:, 0:1], None, ALU.mult), 2)
            chained(s_chain, nc.vector.tensor_scalar(turns, ang, 1.0 / (2 * 3.141592653589793), ROUND,
                                                     ALU.mult, ALU.add), 3)
            chained(s_chain, nc.vector.tensor_scalar(turns, turns, ROUND, None, ALU.subtract), 4)
            chained(s_chain, nc.vector.scalar_tensor_tensor(out=red, in0=turns, scalar=-TWO_PI_A, in1=ang,
                                                            op0=ALU.mult, op1=ALU.add), 5)
            chained(s_chain, nc.vector.scalar_tensor_tensor(out=ang, in0=turns, scalar=-TWO_PI_B, in1=red,
                                                            op0=ALU.mult, op1=ALU.add), 6)
            nc.vector.scalar_tensor_tensor(out=red, in0=turns, scalar=-TWO_PI_C, in1=ang,
                                           op0=ALU.mult, op1=ALU.add).then_inc(s_red, 1)
            dve.wait_ge(s_red, 1)
            nc.vector.tensor_scalar(red, red, -PI_DOWN, PI_DOWN, ALU.max, ALU.min).then_inc(s_red, 1)
            dve.wait_ge(s_red, 2)
            nc.vector.tensor_scalar(turns, red, -1.0, None, ALU.mult).then_inc(s_red, 1)
            dve.wait_ge(s_red, 3)
            nc.vector.tensor_tensor(ang, red, turns, ALU.max).then_inc(s_red, 1)
            dve.wait_ge(s_red, 4)
            nc.vector.tensor_scalar(cosr, ang, -1.0, 1.5707963267948966, ALU.mult, ALU.add).then_inc(s_chain, 1)
            dve.wait_ge(s_sin, 2)

            def tables(n, part):
                dve.wait_ge(s_amp, n)
                nc.vector.tensor_tensor(cs[:, 0, part], cos_t[:, part], amp_t[:, part], ALU.mult)\
                    .then_inc(s_chain, 1)
                nc.vector.tensor_tensor(cs[:, 1, part], sin_t[:, part], amp_t[:, part], ALU.mult)\
                    .then_inc(s_chain, 1)

            tables(1, slice(0, GB))
            dve.wait_ge(s_t1, 1)
            nc.vector.tensor_copy(t1[:, :], ps_u[:, 0:P]).then_inc(s_t1c, 1)
            dve.wait_ge(s_wp, 1)
            nc.vector.tensor_copy(wp[:, :], ps_h[:, 0:P]).then_inc(s_wpc, 1)
            nc.vector.memset(seen[:, 0, :], 0.0).then_inc(s_seen, 1)
            dve.wait_ge(s_chain, 9)

            def build_rot(g):
                dve.wait_ge(s_rotc, g + 1)
                if g >= 2:
                    dve.wait_ge(s_h, g - 1)
                for i in range(GB):
                    b = g * GB + i
                    op = nc.vector.scalar_tensor_tensor(out=rot[:, g % 2, i, :], in0=swap[:, :],
                                                        scalar=cs[:, 1, b:b + 1], in1=rot_c[:, g % 2, i, :],
                                                        op0=ALU.mult, op1=ALU.add)
                op.then_inc(s_rot, 1)

            def add_y(g):
                dve.wait_ge(s_y, g + 1)
                if g >= 2:
                    dve.wait_ge(s_yr, g - 1)
                for b in range(g * GB, g * GB + GB):
                    op = nc.vector.scalar_tensor_tensor(out=yT[:, g % 2, cols(b)], in0=ps_y[:, cols(b)],
                                                        scalar=cond_s[:, b, 2 * P + 1:2 * P + 2],
                                                        in1=x1T[:, g, cols(b)], op0=ALU.add, op1=ALU.add)
                op.then_inc(s_yc, 1)

            def moments(g):
                dve.wait_ge(s_yr, g + 1)
                for i in range(GB):
                    op = nc.vector.bn_stats(stats[:, g % 2, i, :], ps_yr[:, i * P:(i + 1) * P])
                op.then_inc(s_stats, 1)
                dve.wait_ge(s_stats, g + 1)
                for i in range(GB):
                    op = nc.vector.bn_aggr(mv[:, g % 2, i, :], stats[:, g % 2, i, :])
                op.then_inc(s_mv, 1)

            def normalise(g):
                dve.wait_ge(s_rstd, g + 1)
                dve.wait_ge(s_mv, g + 1)
                if g >= 2:
                    dve.wait_ge(s_nT, g - 1)
                for i in range(GB):
                    op = nc.vector.tensor_scalar(yhat[:, g % 2, i * P:(i + 1) * P], ps_yr[:, i * P:(i + 1) * P],
                                                 mv[:, g % 2, i, 0:1], rstd[:, g % 2, i:i + 1],
                                                 ALU.subtract, ALU.mult)
                op.then_inc(s_yhat, 1)

            routed = [0]

            def pick(g):
                def then(op):
                    routed[0] += 1
                    chained(s_route, op, routed[0])

                def wide(t):
                    return t.unsqueeze(2).broadcast_to((P, GB, EXPERTS))

                dve.wait_ge(s_log, g + 1)
                if g >= 2:
                    dve.wait_ge(s_pre, g - 1)
                then(nc.vector.tensor_tensor(logits[:, :, :], ps_log.rearrange("p (b e) -> p b e", b=GB),
                                             br_s[:, :].unsqueeze(1).broadcast_to((P, GB, EXPERTS)),
                                             ALU.add))
                then(nc.vector.tensor_reduce(top[:, :], logits[:, :, :], AX.X, ALU.max))
                then(nc.vector.tensor_tensor(tied[:, :, :], logits[:, :, :], wide(top[:, :]), ALU.is_equal))
                then(nc.vector.tensor_tensor(tied[:, :, :], tied[:, :, :], falling[:, :, :], ALU.mult))
                then(nc.vector.tensor_reduce(first[:, :], tied[:, :, :], AX.X, ALU.max))
                nc.vector.tensor_tensor(onehot[:, g % 2, :, :], falling[:, :, :], wide(first[:, :]),
                                        ALU.is_equal).then_inc(s_onehot, 1)
                dve.wait_ge(s_onehot, g + 1)
                then(nc.vector.tensor_reduce(groupsum[:, :], onehot[:, g % 2, :, :].rearrange("p b e -> p e b"),
                                             AX.X, ALU.add))
                nc.vector.tensor_tensor(seen[:, (g + 1) % 2, :], seen[:, g % 2, :], groupsum[:, :], ALU.add)\
                    .then_inc(s_seen, 1)

            def find_slot(g):
                def then(op):
                    routed[0] += 1
                    chained(s_route, op, routed[0])

                dve.wait_ge(s_pre, g + 1)
                then(nc.vector.tensor_tensor(place[:, :, :], ps_pre.rearrange("p (b e) -> p b e", b=GB),
                                             area[:, :].unsqueeze(1).broadcast_to((P, GB, EXPERTS)),
                                             ALU.add))
                then(nc.vector.tensor_tensor(place[:, :, :], place[:, :, :], onehot[:, g % 2, :, :], ALU.mult))
                if g == SOONER - 1:
                    nc.vector.tensor_copy(cnt_i[:, :], ps_cnt[0:1, :]).then_inc(s_counted, 1)
                with nc.allow_low_precision(reason="row numbers are integers below 2**24"):
                    nc.vector.tensor_reduce(slot[:, g * GB:(g + 1) * GB], place[:, :, :], AX.X, ALU.add)\
                        .then_inc(s_slot, 1)

            tabled = [0]

            def table(op):
                tabled[0] += 1
                chained(s_table, op, tabled[0])

            def is_past(n):
                table(nc.vector.tensor_tensor_scan(cum[:, :], ones_8[:, :], nt[:, :], 0.0, ALU.mult, ALU.add))
                table(nc.vector.tensor_tensor(past[:, 0:n, :], cum[:, :].unsqueeze(1).broadcast_to((1, n, EXPERTS)),
                                              tau[:, 0:n].unsqueeze(2).broadcast_to((1, n, EXPERTS)), ALU.is_le))

            def experts_of(first, n):
                table(nc.vector.tensor_reduce(tsum[:, 0:n], past[:, 0:n, :], AX.X, ALU.add))
                table(nc.vector.tensor_scalar(tile_e[:, first:first + n], tsum[:, 0:n], float(EXPERTS - 1), None,
                                              ALU.min))

            def jumps(n):
                table(nc.vector.tensor_tensor(pastw[:, 0:n, :], past[:, 0:n, :],
                                              jump[:, :].unsqueeze(1).broadcast_to((1, n, EXPERTS)), ALU.mult))
                table(nc.vector.tensor_reduce(tsum[:, 0:n], pastw[:, 0:n, :], AX.X, ALU.add))

            def sooner_tiles():
                dve.wait_ge(s_counted, 1)
                table(nc.vector.tensor_scalar(nt_i[:, :], cnt_i[:, :], 7, None, ALU.logical_shift_right))
                table(nc.vector.tensor_copy(nt[:, :], nt_i[:, :]))
                table(nc.vector.tensor_scalar(jump[:, :], nt[:, :], -float(P), float(PITCH), ALU.mult, ALU.add))
                is_past(SOON)
                experts_of(0, SOON)
                jumps(SOON)
                nc.vector.tensor_tensor(tile_r[:, 0:SOON], tsum[:, 0:SOON], tau128[:, 0:SOON], ALU.add)\
                    .then_inc(s_tiles, 1)
                dve.wait_ge(s_tiles, 1)

            def tiles_taken():
                table(nc.vector.memset(capped[:, 0:1], 0.0))
                table(nc.vector.memset(taken[:, EXPERTS:], 0.0))
                table(nc.vector.tensor_scalar(capped[:, 1:], cum[:, :], float(SOON), None, ALU.min))
                table(nc.vector.tensor_tensor(taken[:, 0:EXPERTS], capped[:, 1:], capped[:, 0:EXPERTS],
                                              ALU.subtract))
                table(nc.vector.tensor_tensor(step_up[:, :], taken[:, 1:], taken[:, 0:EXPERTS], ALU.subtract))
                table(nc.vector.tensor_scalar(step_up[:, :], step_up[:, :], float(P), float(PITCH), ALU.mult,
                                              ALU.add))
                table(nc.vector.tensor_scalar(taken_0[:, :], taken[:, 0:1], float(P), None, ALU.mult))

            def later_tiles(part):
                if part == 0:
                    table(nc.vector.tensor_scalar(cnt_i[:, :], ps_cnt[0:1, :], float(P - 1), None, ALU.add))
                    table(nc.vector.tensor_scalar(nt_i[:, :], cnt_i[:, :], 7, None, ALU.logical_shift_right))
                    table(nc.vector.tensor_tensor(nt[:, :], nt_i[:, :], taken[:, 0:EXPERTS], ALU.subtract))
                    table(nc.vector.scalar_tensor_tensor(out=jump[:, :], in0=nt[:, :], scalar=-float(P),
                                                         in1=step_up[:, :], op0=ALU.mult, op1=ALU.add))
                elif part == 1:
                    is_past(LATER)
                elif part == 2:
                    experts_of(SOON, LATER)
                else:
                    jumps(LATER)
                    table(nc.vector.scalar_tensor_tensor(out=tsum[:, 0:LATER], in0=tsum[:, 0:LATER],
                                                         scalar=taken_0[:, 0:1], in1=tau128[:, 0:LATER],
                                                         op0=ALU.add, op1=ALU.add))
                    nc.vector.tensor_scalar(tile_r[:, SOON:TILES], tsum[:, 0:LATER], float(DUMMY), None, ALU.min)\
                        .then_inc(s_tiles, 1)
                    dve.wait_ge(s_tiles, 2)

            def stage_expert(k, e):
                nc.vector.tensor_scalar(stage[:, k, :], w1_s[:, bass.ds(e, 1), :].rearrange("p a f -> p (a f)"),
                                        1.0, None, ALU.mult).then_inc(s_stage, 1)

            def residual(k, arrivals, staged, freed=None):
                dve.wait_ge(d_rows[k], arrivals)
                dve.wait_ge(s_stage, staged)
                if freed is not None:
                    dve.wait_ge(s_res, freed)
                nc.vector.tensor_tensor(resid[:, k, :], rows[:, k, P:2 * P], stage[:, k, EB:EW], ALU.add)\
                    .then_inc(s_resid, 1)

            for stage_name, g in in_turn({"moments": 3, "pick": 5, "y": 2, "slot": 5, "rot": -1, "normalise": 3}):
                if stage_name == "rot" and g == 0:
                    dve.wait_ge(s_const, 9)
                if stage_name == "rot" and g == 1:
                    tables(2, slice(GB, BATCHES))
                    dve.wait_ge(s_chain, 11)
                if stage_name == "y":
                    dve.wait_ge(d_cond[g], 16 * GB)
                if stage_name == "pick" and g == 0:
                    dve.wait_ge(s_const, N_CONST)
                    dve.wait_ge(d_small, 48)
                {"rot": build_rot, "y": add_y, "moments": moments, "normalise": normalise, "pick": pick,
                 "slot": find_slot}[stage_name](g)
                if (stage_name, g) == ("normalise", GROUPS - 1):
                    sooner_tiles()
                if (stage_name, g) == ("slot", GROUPS - 2):
                    dve.wait_ge(d_experts, 48)
                    for t, e in enumerate(loaded(DVE, tile_e, 0, EXPERTS - 1)):
                        stage_expert(t, e)
                    tiles_taken()
            nc.vector.tensor_tensor(pad_row[:, :], ps_cnt[0:1, :], area[0:1, :], ALU.add).then_inc(s_padrow, 1)

            def relu_hi(k, tiles_done):
                dve.wait_ge(s_hhi, tiles_done)
                for c in range(CHUNKS // 2, CHUNKS):
                    op = nc.vector.tensor_scalar(hT[:, k, c * P:(c + 1) * P], ps_hi[:, c * P:(c + 1) * P],
                                                 stage[:, k, FF + c:FF + c + 1], 0.0, ALU.add, ALU.max)
                op.then_inc(s_hhic, 1)

            def result(k, tiles_done, stored=None):
                dve.wait_ge(s_out, tiles_done)
                dve.wait_ge(s_resid, tiles_done)
                if stored is not None:
                    dve.wait_ge(d_res[k], stored)
                nc.vector.tensor_tensor(res[:, k, :], ps_out[k][:, 0:P], resid[:, k, :], ALU.add)\
                    .then_inc(s_res, 1)

            def step(t, e):
                relu_hi(t % 3, t + 1)
                if e is not None:
                    dve.wait_ge(s_hloc, t + 1)
                    dve.wait_ge(s_hhic, t + 1)
                    dve.wait_ge(s_resid, t + 1)
                    stage_expert(t % 3, e)
                if t >= 1:
                    result((t - 1) % 3, t, 16 * ((t - 1) // 3) if t > 3 else None)
                if t + 1 < TILES:
                    residual((t + 1) % 3, 16 * ((t + 1) // 3 + 1), t + 2, t - 1 if t >= 2 else None)

            residual(0, 16, 1)
            second = loaded(DVE, tile_e, 3, EXPERTS - 1)
            for t in range(4):
                step(t, second[t] if t < 3 else loaded(DVE, tile_e, 6, EXPERTS - 1)[0])
                later_tiles(t)
            with dve.Fori(1, TILES // 3 - 2) as j:
                for k in range(3):
                    relu_hi((k + 1) % 3, j * 3 + (k + 2))
                    if k == 0:
                        expert = loaded(DVE, tile_e, j * 3 + 4, EXPERTS - 1)
                    dve.wait_ge(s_hloc, j * 3 + (k + 2))
                    dve.wait_ge(s_hhic, j * 3 + (k + 2))
                    dve.wait_ge(s_resid, j * 3 + (k + 2))
                    stage_expert((k + 1) % 3, expert[k])
                    result(k, j * 3 + (k + 1), j * 16)
                    residual((k + 2) % 3, j * 16 + (16 if k == 0 else 32), j * 3 + (k + 3), j * 3 + k)
            last = loaded(DVE, tile_e, TILES - 3, EXPERTS - 1)[1:]
            for t in range(TILES - 5, TILES):
                step(t, last[t - TILES + 5] if t < TILES - 3 else None)
            result((TILES - 1) % 3, TILES, 16 * ((TILES - 1) // 3))


def kernel(**inputs):
    import numpy as np
    import concourse.bacc as _bacc
    from concourse import mybir as _mybir
    from concourse.bass_utils import run_bass_kernel_spmd as _run

    a = {k: np.asarray(v) for k, v in inputs.items()}
    laid = {
        "xT": a["x"].transpose(2, 0, 1).reshape(P, TOKENS),
        "w0": np.stack([a["L0_ffn_weight"].T, a["L0_ffn_aux_weight1"].T, a["L0_ffn_aux_weight2"]], axis=1),
        "bias0": a["L0_ffn_bias"],
        "amp": np.repeat(a["L0_cond_amplitudes"], 2),
        "freq": np.repeat(a["L0_cond_frequencies"], 2),
        "delta": a["condB_deltat"],
        "prof": a["itok_B_0_6"],
        "cond": np.concatenate([a["L1_cond_down_w"], a["L1_cond_up_w"], a["L1_cond_down_b"][:, :, None],
                                a["L1_cond_up_b"][:, :, None], a["L1_cond_ln_g"][:, :, None],
                                a["L1_cond_ln_b"][:, :, None]], axis=2),
        "wr": a["L1_ffn_Wr"].T,
        "br": a["L1_ffn_br"],
        "w1": np.concatenate([a["L1_ffn_W1"].transpose(2, 0, 1),
                              a["L1_ffn_b1"].reshape(EXPERTS, CHUNKS, P).transpose(2, 0, 1)], axis=2),
        "w2": a["L1_ffn_W2"].reshape(EXPERTS, P, CHUNKS, P).transpose(3, 0, 2, 1),
        "b2": a["L1_ffn_b2"],
    }
    nc = _bacc.Bacc("TRN2", target_bir_lowering=False, num_devices=1)
    arrays, args = {}, []
    for name, v in laid.items():
        v = np.ascontiguousarray(v)
        arrays[f"in_{name}"] = v
        args.append(nc.dram_tensor(f"in_{name}", v.shape, _mybir.dt.from_np(v.dtype), kind="ExternalInput").ap())
    args.append(nc.dram_tensor("out_0", (BATCHES, P, P), _mybir.dt.float32, kind="ExternalOutput").ap())
    adaln_moe(nc, *args)
    r = _run(nc, [arrays], core_ids=[0])
    return r.results[0]["out_0"]
```

```python
from contextlib import ExitStack

import concourse.bass as bass
from concourse import mybir

P = 128
BATCHES = 32
TOKENS = BATCHES * P
EXPERTS = 8
PROFILES = 8
FF = 512
CHUNKS = FF // P
GB = 4
GROUPS = BATCHES // GB
GN = GB * P
PITCH = TOKENS + P
DUMMY = EXPERTS * PITCH
TILES = TOKENS // P + EXPERTS - 1
SOONER = 4
SOON = SOONER * GB - EXPERTS + 1
LATER = TILES - SOON
ROW = 260
ID = 2 * P
NO_TOKEN = float(1 << 20)
CW = 260
EB = FF + CHUNKS
EW = EB + P
EPS = 1e-5

F32 = mybir.dt.float32
I32 = mybir.dt.int32
BF16 = mybir.dt.bfloat16
ALU = mybir.AluOpType
ACT = mybir.ActivationFunctionType
AX = mybir.AxisListType

TWO_PI_A, TWO_PI_B, TWO_PI_C = 6.28125, 0.0019340515136718750, 1.2556659146e-06
PI_DOWN = 3.1415925
SP, PE, DVE = mybir.EngineType.SP, mybir.EngineType.PE, mybir.EngineType.DVE
PARTS = [slice(0, 8), slice(8, 16), slice(16, BATCHES)]
ROUND = 1.5 * 2.0 ** 23


def adaln_moe(nc, xT, w0, bias0, amp, freq, delta, prof, cond, wr, br, w1, w2, b2, out):
    rows_d = nc.dram_tensor("expert_rows", (DUMMY + P, ROW), F32).ap()
    out_rows = out.rearrange("b s d -> (b s) d")

    with ExitStack() as ctx:
        def sb(name, shape, dt=F32):
            return ctx.enter_context(nc.sbuf_tensor(name, shape, dt))

        def sem(name):
            return ctx.enter_context(nc.semaphore(name))

        w0_s = sb("w0_s", [P, 3, P])
        t1 = sb("t1", [P, P])
        wp = sb("wp", [P, P])
        bias0_s = sb("bias0_s", [P, 1])
        prof_s = sb("prof_s", [1, BATCHES], I32)
        amp_s = sb("amp_s", [P, 1])
        freq_s = sb("freq_s", [P, 1])
        delta_s = sb("delta_s", [P, BATCHES])
        cond_s = sb("cond_s", [P, BATCHES, CW])
        wr_s = sb("wr_s", [P, EXPERTS])
        br_s = sb("br_s", [P, EXPERTS])
        w1_s = sb("w1_s", [P, EXPERTS, EW])
        w2_s = sb("w2_s", [P, EXPERTS, CHUNKS, P])

        ident = sb("ident", [P, P])
        swap = sb("swap", [P, P])
        before = sb("before", [P, P], BF16)
        ones_b = sb("ones_b", [P, P], BF16)
        ones_8 = sb("ones_8", [1, EXPERTS])
        neg_half = sb("neg_half", [P, GB])
        falling = sb("falling", [P, GB, EXPERTS])
        area = sb("area", [P, EXPERTS])
        tau = sb("tau", [1, TILES])
        tau128 = sb("tau128", [1, TILES])
        pad = sb("pad", [P, ROW])

        trig = sb("trig", [P, 8, BATCHES])
        ang, turns, red, cosr, sin_t, cos_t, amp_t, amp_b = (trig[:, i, :] for i in range(8))
        cs = sb("cs", [P, 2, BATCHES])
        rot_c = sb("rot_c", [P, 2, GB, P])
        rot = sb("rot", [P, 2, GB, P])

        x1T = sb("x1T", [P, GROUPS, GN])
        u = sb("u", [P, 2, GN])
        warm = sb("warm", [P, 2])
        tanh_s = sb("tanh_s", [P, 2, GN])
        zT = sb("zT", [P, 2, GN])
        yT = sb("yT", [P, 2, GN])
        yhat = sb("yhat", [P, 2, GN])
        xnT = sb("xnT", [P, 2, GN])
        stats = sb("stats", [P, 2, GB, 6])
        mv = sb("mv", [P, 2, GB, 2])
        vareps = sb("vareps", [P, 2, GB])
        rstd = sb("rstd", [P, 2, GB])
        payload = sb("payload", [P, BATCHES, ROW])

        logits = sb("logits", [P, GB, EXPERTS])
        top = sb("top", [P, GB])
        tied = sb("tied", [P, GB, EXPERTS])
        first = sb("first", [P, GB])
        onehot = sb("onehot", [P, 2, GB, EXPERTS], BF16)
        seen = sb("seen", [P, 2, EXPERTS], BF16)
        groupsum = sb("groupsum", [P, EXPERTS])
        place = sb("place", [P, GB, EXPERTS])
        slot = sb("slot", [P, BATCHES], I32)

        cnt_i = sb("cnt_i", [1, EXPERTS], I32)
        nt_i = sb("nt_i", [1, EXPERTS], I32)
        nt = sb("nt", [1, EXPERTS])
        capped = sb("capped", [1, 1 + EXPERTS])
        taken = sb("taken", [1, EXPERTS + 1])
        step_up = sb("step_up", [1, EXPERTS])
        taken_0 = sb("taken_0", [1, 1])
        cum = sb("cum", [1, EXPERTS])
        jump = sb("jump", [1, EXPERTS])
        past = sb("past", [1, TILES, EXPERTS])
        pastw = sb("pastw", [1, TILES, EXPERTS])
        tsum = sb("tsum", [1, TILES])
        esum = sb("esum", [1, TILES])
        pad_row = sb("pad_row", [1, EXPERTS], I32)
        tile_e = sb("tile_e", [1, TILES], I32)
        tile_r = sb("tile_r", [1, TILES], I32)

        rows = sb("rows", [P, 3, ROW])
        ids = sb("ids", [P, 6], I32)
        zero_i = sb("zero_i", [P, 1], I32)
        tileT = sb("tileT", [P, 3, P])
        stage = sb("stage", [P, 3, EW])
        hT = sb("hT", [P, 3, FF])
        resid = sb("resid", [P, 3, P])
        res = sb("res", [P, 3, P])

        bank = [ctx.enter_context(nc.psum_tensor(f"bank{i}", [P, GN], F32)) for i in range(8)]
        ps_u, ps_h, ps_z, ps_y, ps_r = bank[0], bank[1], bank[2], bank[3], bank[7]
        ps_yr = (bank[4], bank[6])
        ps_n = bank[5]
        ps_nr = ps_z
        ps_x1 = ps_u
        ps_log = ps_r[:, 0:GB * EXPERTS]
        ps_pre = ps_r[:, 64:64 + GB * EXPERTS]
        ps_cnt = ps_r[:, 128:128 + EXPERTS]
        ps_t = bank[3]
        ps_lo, ps_hi = bank[0], bank[1]
        ps_out = (bank[4], bank[6], bank[5])

        d_w0 = sem("d_w0")
        d_trig = sem("d_trig")
        d_prof = sem("d_prof")
        d_small = sem("d_small")
        d_x = [sem(f"d_x{g}") for g in range(GROUPS)]
        d_cond = [sem(f"d_cond{g}") for g in range(GROUPS)]
        d_experts = sem("d_experts")
        d_scatter = sem("d_scatter")
        d_late = sem("d_late")
        d_pads = sem("d_pads")
        d_dummy = sem("d_dummy")
        d_rows = [sem(f"d_rows{k}") for k in range(3)]
        d_res = [sem(f"d_res{k}") for k in range(3)]

        s_const = sem("s_const")
        s_t1 = sem("s_t1")
        s_t1c = sem("s_t1c")
        s_wp = sem("s_wp")
        s_wpc = sem("s_wpc")
        s_chain = sem("s_chain")
        s_red = sem("s_red")
        s_amp = sem("s_amp")
        s_sin = sem("s_sin")
        s_rotc = sem("s_rotc")
        s_rot = sem("s_rot")
        s_u = sem("s_u")
        s_uc = sem("s_uc")
        s_h = sem("s_h")
        s_tanh = sem("s_tanh")
        s_x1T = sem("s_x1T")
        s_x1 = sem("s_x1")
        s_x1c = sem("s_x1c")
        s_z = sem("s_z")
        s_zc = sem("s_zc")
        s_y = sem("s_y")
        s_yc = sem("s_yc")
        s_yr = sem("s_yr")
        s_stats = sem("s_stats")
        s_mv = sem("s_mv")
        s_var = sem("s_var")
        s_rstd = sem("s_rstd")
        s_yhat = sem("s_yhat")
        s_nT = sem("s_nT")
        s_nTc = sem("s_nTc")
        s_nr = sem("s_nr")
        s_nrc = sem("s_nrc")
        s_log = sem("s_log")
        s_pick = sem("s_pick")
        s_groupsum = sem("s_groupsum")
        s_place = sem("s_place")
        s_onehot = sem("s_onehot")
        s_seen = sem("s_seen")
        s_pre = sem("s_pre")
        s_slot = sem("s_slot")
        s_counted = sem("s_counted")
        s_padrow = sem("s_padrow")
        s_table = sem("s_table")
        s_tiles = sem("s_tiles")
        s_experts = sem("s_experts")
        s_tT = sem("s_tT")
        s_tTc = sem("s_tTc")
        s_stage = sem("s_stage")
        s_hlo = sem("s_hlo")
        s_hhi = sem("s_hhi")
        s_hloc = sem("s_hloc")
        s_hhic = sem("s_hhic")
        s_out = sem("s_out")
        s_res = sem("s_res")
        s_taken = sem("s_taken")
        s_resid = sem("s_resid")

        PICKS = 5
        N_CONST = 18
        N_ALL = N_CONST + 1
        block = ctx.enter_context(nc.Block())

        def loaded(engine, table, first, high, n=3):
            at = slice(first, first + n) if isinstance(first, int) else bass.ds(first, n)
            return nc.values_load_multi_w_load_instructions(
                table[0:1, at], engines=(engine,), min_val=0, max_val=high,
                skip_runtime_bounds_check_because="the table's values are in this range as they are made")[1]

        def cols(b):
            return slice(b % GB * P, b % GB * P + P)

        def in_turn(lags):
            for t in range(min(lags.values()), GROUPS + max(lags.values())):
                for stage_name, lag in lags.items():
                    if 0 <= t - lag < GROUPS:
                        yield stage_name, t - lag

        @block.sync
        def _(sp):
            sp.dma_start(delta_s[:, :], delta.partition_broadcast(P)).then_inc(d_trig, 16)
            sp.dma_start(freq_s[:, :], freq.rearrange("(p a) -> p a", a=1)).then_inc(d_trig, 16)
            sp.dma_start(amp_s[:, :], amp.rearrange("(p a) -> p a", a=1)).then_inc(d_trig, 16)
            sp.dma_start(x1T[:, 0, :], xT[:, 0:GN]).then_inc(d_x[0], 16)
            sp.dma_start(prof_s[:, :], prof.rearrange("(a n) -> a n", a=1)).then_inc(d_prof, 16)
            sp.dma_start(x1T[:, 1, :], xT[:, GN:2 * GN]).then_inc(d_x[1], 16)
            sp.wait_ge(d_prof, 16)
            for g in range(GROUPS):
                for b in range(g * GB, g * GB + GB):
                    p = sp.value_load(prof_s[0:1, b:b + 1], min_val=0, max_val=PROFILES - 1)
                    sp.dma_start(cond_s[:, b, :], cond[bass.ds(p, 1), :, :].rearrange("a p c -> (a p) c"))\
                        .then_inc(d_cond[g], 16)
                if g + 2 < GROUPS:
                    sp.dma_start(x1T[:, g + 2, :], xT[:, (g + 2) * GN:(g + 3) * GN]).then_inc(d_x[g + 2], 16)
            sp.dma_start(w1_s[:, :, 0:EB], w1).then_inc(d_experts, 16)
            sp.dma_start(w1_s[:, :, EB:EW], b2.partition_broadcast(P)).then_inc(d_experts, 16)
            sp.dma_start(w2_s[:, :, :, :], w2).then_inc(d_experts, 16)

            def load_rows(k, r):
                sp.dma_start(rows[:, k, :], rows_d[bass.ds(r, P), :]).then_inc(d_rows[k], 16)

            sp.wait_ge(s_tiles, 1)
            starts = loaded(SP, tile_r, 0, DUMMY)
            sp.wait_ge(d_scatter, 16 * SOONER * GB)
            for t in range(3):
                load_rows(t, starts[t])

            def slot_free(tiles_done):
                sp.wait_ge(s_tT, tiles_done)
                sp.wait_ge(s_taken, tiles_done)
                sp.wait_ge(s_resid, tiles_done)

            starts = loaded(SP, tile_r, 3, DUMMY)
            for k in range(3):
                slot_free(k + 1)
                load_rows(k, starts[k])
            starts = loaded(SP, tile_r, 6, DUMMY)
            for k in range(3):
                slot_free(k + 4)
                load_rows(k, starts[k])
                if k == 0:
                    sp.wait_ge(s_padrow, 1)
                    ends = loaded(SP, pad_row, 0, DUMMY - P, EXPERTS)
                for e in range(0, 4) if k == 0 else range(4, EXPERTS) if k == 1 else ():
                    sp.dma_start(rows_d[bass.ds(ends[e], P), :], pad[:, :]).then_inc(d_pads, 16)

            def load_more(first, last):
                with sp.Fori(first, last) as j:
                    starts = loaded(SP, tile_r, j * 3 + 3, DUMMY)
                    for k in range(3):
                        slot_free(j * 3 + (k + 1))
                        load_rows(k, starts[k])

            sp.wait_ge(s_tiles, 2)
            sp.wait_ge(d_late, 16 * (BATCHES - SOONER * GB))
            sp.wait_ge(d_pads, 16 * EXPERTS)
            sp.wait_ge(d_dummy, 16)
            load_more(SOON // 3 - 1, TILES // 3 - 1)

        @block.gpsimd
        def _(pool):
            pool.memset(ident[:, :], 0.0).then_inc(s_const, 1)
            pool.memset(swap[:, :], 0.0).then_inc(s_const, 1)
            pool.memset(pad[:, :], 0.0).then_inc(s_const, 1)
            pool.memset(before[:, :], 1.0).then_inc(s_const, 1)
            pool.memset(ones_b[:, :], 1.0).then_inc(s_const, 1)
            pool.memset(neg_half[:, :], -0.5).then_inc(s_const, 1)
            pool.wait_ge(s_const, 6)
            pool.affine_select(out=ident[:, :], in_=ident[:, :], compare_op=ALU.not_equal, fill=1.0, base=0,
                               pattern=[[-1, P]], channel_multiplier=1).then_inc(s_const, 1)
            pairs = swap[:, :].rearrange("p (f two) -> p f two", two=2)
            pool.affine_select(out=pairs[:, :, 0], in_=pairs[:, :, 0], compare_op=ALU.not_equal, fill=-1.0,
                               base=-1, pattern=[[-2, P // 2]], channel_multiplier=1).then_inc(s_const, 1)
            pool.affine_select(out=pairs[:, :, 1], in_=pairs[:, :, 1], compare_op=ALU.not_equal, fill=1.0,
                               base=0, pattern=[[-2, P // 2]], channel_multiplier=1).then_inc(s_const, 1)
            pool.wait_ge(d_trig, 48)
            pool.wait_ge(s_chain, 1)
            for part in PARTS[:2]:
                pool.tensor_tensor(amp_t[:, part], amp_b[:, part], delta_s[:, part], ALU.pow).then_inc(s_amp, 1)

            def cos_part(g):
                pool.wait_ge(s_chain, 9 if g < 2 else 11 if g < 4 else 13)
                if g >= 2:
                    pool.wait_ge(s_rot, GB * (g - 1))
                pool.tensor_tensor(rot_c[:, g % 2, :, :], ident[:, :].unsqueeze(1).broadcast_to((P, GB, P)),
                                   cs[:, 0, g * GB:(g + 1) * GB].unsqueeze(2).broadcast_to((P, GB, P)),
                                   ALU.mult).then_inc(s_rotc, 1)

            cos_part(0)
            cos_part(1)
            pool.tensor_tensor(amp_t[:, PARTS[2]], amp_b[:, PARTS[2]], delta_s[:, PARTS[2]], ALU.pow)\
                .then_inc(s_amp, 1)
            def routing_constants():
                pool.affine_select(out=before[:, :], in_=before[:, :], compare_op=ALU.is_gt, fill=0.0, base=0,
                                   pattern=[[1, P]], channel_multiplier=-1).then_inc(s_const, 1)
                pool.memset(pad[:, ID:ID + 1].bitcast(I32), int(NO_TOKEN)).then_inc(s_const, 1)
                pool.iota(falling[:, :, :], pattern=[[0, GB], [-1, EXPERTS]], base=EXPERTS, channel_multiplier=0,
                          allow_small_or_imprecise_dtypes=True).then_inc(s_const, 1)
                pool.iota(area[:, :], pattern=[[PITCH, EXPERTS]], base=0, channel_multiplier=0,
                          allow_small_or_imprecise_dtypes=True).then_inc(s_const, 1)
                pool.iota(tau[:, :], pattern=[[1, TILES]], base=0, channel_multiplier=0,
                          allow_small_or_imprecise_dtypes=True).then_inc(s_const, 1)
                pool.iota(tau128[:, :], pattern=[[P, TILES]], base=0, channel_multiplier=0,
                          allow_small_or_imprecise_dtypes=True).then_inc(s_const, 1)
                pool.memset(payload[:, :, ID:ROW], 0.0).then_inc(s_const, 1)
                pool.memset(ones_8[:, :], 1.0).then_inc(s_const, 1)
                pool.memset(zero_i[:, :], 0).then_inc(s_const, 1)
                pool.wait_ge(s_const, N_CONST)
                pool.iota(payload[:, :, ID].bitcast(I32), pattern=[[P, BATCHES]], base=0, channel_multiplier=1)\
                    .then_inc(s_const, 1)
                pool.dma_start(rows_d[DUMMY:DUMMY + P, :], pad[:, :]).then_inc(d_dummy, 16)

            def add_x(g):
                pool.wait_ge(s_tanh, g + 1)
                pool.wait_ge(s_u, g + 1)
                pool.tensor_tensor(x1T[:, g, :], x1T[:, g, :], tanh_s[:, g % 2, :], ALU.add).then_inc(s_x1T, 1)

            def deviation(g):
                pool.wait_ge(s_var, g + 1)
                pool.tensor_tensor(rstd[:, g % 2, :], vareps[:, g % 2, :], neg_half[:, :], ALU.pow)\
                    .then_inc(s_rstd, 1)

            def scatter(g, batches=range(GB)):
                pool.wait_ge(s_slot, g + 1)
                pool.wait_ge(s_nrc, g + 1)
                pool.wait_ge(s_x1c, g + 1)
                pool.wait_ge(s_const, N_ALL)
                for b in (g * GB + i for i in batches):
                    pool.indirect_dma_start(
                        out=rows_d, out_offset=bass.IndirectOffsetOnAxis(ap=slot[:, b:b + 1], axis=0),
                        in_=payload[:, b, :], in_offset=None)\
                        .then_inc(d_scatter if g < SOONER else d_late, 16)

            last_token = pool.to_reg(TOKENS - 1)

            def take_ids(k, i, arrivals):
                pool.wait_ge(d_rows[k], arrivals)
                pool.tensor_tensor(ids[:, i:i + 1], rows[:, k, ID:ID + 1].bitcast(I32), zero_i[:, :], ALU.add)\
                    .then_inc(s_taken, 1)

            def store(k, i):
                pool.indirect_dma_start(
                    out=out_rows, out_offset=bass.IndirectOffsetOnAxis(ap=ids[:, i:i + 1], axis=0),
                    in_=res[:, k, :], in_offset=None, bounds_check=last_token, oob_is_err=False)\
                    .then_inc(d_res[k], 16)

            for stage_name, g in in_turn({"cos": -2, "dev": 3, "add": 0, "scatter": 5}):
                if (stage_name, g) == ("scatter", GROUPS - 3):
                    for t in range(3):
                        take_ids(t, t, 16)
                if stage_name == "cos" and g < 2 or stage_name == "scatter" and g > GROUPS - 3:
                    continue
                {"cos": cos_part, "add": add_x, "dev": deviation, "scatter": scatter}[stage_name](g)
                if (stage_name, g) == ("add", 0):
                    routing_constants()

            def result_ready(t):
                pool.wait_ge(s_res, t + 1)
                pool.wait_ge(s_taken, t + 1)

            take_ids(0, 3, 32)
            scatter(GROUPS - 2, (0, 1))
            result_ready(0)
            store(0, 0)
            scatter(GROUPS - 2, (2, 3))
            take_ids(1, 4, 32)
            result_ready(1)
            store(1, 1)
            take_ids(2, 5, 32)
            scatter(GROUPS - 1)
            result_ready(2)
            store(2, 2)
            with pool.Fori(0, (TILES - 6) // 6) as j:
                for q in range(6):
                    pool.wait_ge(s_res, j * 6 + (q + 4))
                    pool.wait_ge(s_taken, j * 6 + (q + 6))
                    take_ids(q % 3, q, j * 32 + 16 * (q // 3 + 3))
                    store(q % 3, (q + 3) % 6)
            for t in range(6 + (TILES - 6) // 6 * 6, TILES + 3):
                result_ready(t - 3)
                if t < TILES:
                    take_ids(t % 3, t % 6, 16 * (t // 3 + 1))
                store((t - 3) % 3, (t - 3) % 6)
            for k in range(3):
                pool.wait_ge(d_res[k], 16 * (TILES // 3))

        @block.scalar
        def _(act):
            act.dma_start(w0_s[:, :, :], w0).then_inc(d_w0, 16)
            act.wait_ge(s_const, 6)
            nc.scalar.activation(warm[:, 0:1], neg_half[:, 0:1], ACT.Sin)
            act.dma_start(bias0_s[:, :], bias0.rearrange("(p a) -> p a", a=1)).then_inc(d_small, 16)
            act.dma_start(wr_s[:, :], wr).then_inc(d_small, 16)
            act.dma_start(br_s[:, :], br.partition_broadcast(P)).then_inc(d_small, 16)
            act.wait_ge(s_t1, 1)
            nc.scalar.activation(t1[:, :], ps_u[:, 0:P], ACT.Copy).then_inc(s_t1c, 1)
            act.wait_ge(s_wp, 1)
            nc.scalar.activation(wp[:, :], ps_h[:, 0:P], ACT.Copy).then_inc(s_wpc, 1)
            act.wait_ge(s_chain, 7)
            nc.scalar.activation(sin_t, red, ACT.Sin).then_inc(s_sin, 1)
            nc.scalar.activation(cos_t, cosr, ACT.Sin).then_inc(s_sin, 1)
            nc.scalar.activation(warm[:, 1:2], cosr[:, 0:1], ACT.Tanh)

            def copy_u(g):
                act.wait_ge(s_u, g + 1)
                if g >= 2:
                    act.wait_ge(s_h, g - 1)
                nc.scalar.activation(u[:, g % 2, :], ps_u[:, :], ACT.Copy).then_inc(s_uc, 1)

            def tanh(g):
                act.wait_ge(s_h, g + 1)
                if g >= 2:
                    act.wait_ge(s_x1T, g - 1)
                nc.scalar.activation(tanh_s[:, g % 2, :], ps_h[:, :], ACT.Tanh, bias=bias0_s[:, 0:1])\
                    .then_inc(s_tanh, 1)

            def copy_x1(g):
                act.wait_ge(s_x1, g + 1)
                nc.scalar.activation(payload[:, g * GB:(g + 1) * GB, P:2 * P],
                                     ps_x1[:, :].rearrange("p (b d) -> p b d", b=GB), ACT.Copy).then_inc(s_x1c, 1)

            def relu_z(g):
                act.wait_ge(s_z, g + 1)
                if g >= 2:
                    act.wait_ge(s_y, g - 1)
                for b in range(g * GB, g * GB + GB):
                    op = nc.scalar.activation(zT[:, g % 2, cols(b)], ps_z[:, cols(b)], ACT.Relu,
                                              bias=cond_s[:, b, 2 * P:2 * P + 1])
                op.then_inc(s_zc, 1)

            def gain(g):
                act.wait_ge(s_nT, g + 1)
                if g >= 2:
                    act.wait_ge(s_log, g - 1)
                for b in range(g * GB, g * GB + GB):
                    op = nc.scalar.activation(xnT[:, g % 2, cols(b)], ps_n[:, cols(b)], ACT.Identity,
                                              scale=cond_s[:, b, 2 * P + 2:2 * P + 3],
                                              bias=cond_s[:, b, 2 * P + 3:2 * P + 4])
                op.then_inc(s_nTc, 1)

            def copy_xn(g):
                act.wait_ge(s_nr, g + 1)
                nc.scalar.activation(payload[:, g * GB:(g + 1) * GB, 0:P],
                                     ps_nr[:, :].rearrange("p (b d) -> p b d", b=GB), ACT.Copy).then_inc(s_nrc, 1)

            def copy_tile(k, tiles_done):
                act.wait_ge(s_tT, tiles_done)
                nc.scalar.activation(tileT[:, k, :], ps_t[:, k * P:(k + 1) * P], ACT.Copy).then_inc(s_tTc, 1)

            def relu_lo(k, tiles_done):
                act.wait_ge(s_hlo, tiles_done)
                for c in range(CHUNKS // 2):
                    op = nc.scalar.activation(hT[:, k, c * P:(c + 1) * P], ps_lo[:, c * P:(c + 1) * P],
                                              ACT.Relu, bias=stage[:, k, FF + c:FF + c + 1])
                op.then_inc(s_hloc, 1)

            act.wait_ge(d_small, 48)
            for stage_name, g in in_turn({"u": 0, "gain": 4, "z": 1, "tanh": 0, "x1": 1, "xn": 4}):
                if (stage_name, g) == ("xn", GROUPS - 2):
                    copy_tile(0, 1)
                    relu_lo(0, 1)
                    copy_tile(1, 2)
                if (stage_name, g) == ("xn", GROUPS - 1):
                    relu_lo(1, 2)
                    copy_tile(2, 3)
                if stage_name == "z":
                    act.wait_ge(d_cond[g], 16 * GB)
                {"u": copy_u, "tanh": tanh, "x1": copy_x1, "z": relu_z, "gain": gain, "xn": copy_xn}[stage_name](g)

            with act.Fori(0, TILES // 3 - 1) as j:
                for k in range(3):
                    relu_lo((k + 2) % 3, j * 3 + (k + 3))
                    copy_tile(k, j * 3 + (k + 4))
            relu_lo((TILES - 1) % 3, TILES)

        @block.tensor
        def _(pe):
            pe.wait_ge(d_w0, 16)
            nc.tensor.matmul(ps_u[:, 0:P], w0_s[:, 1, :], w0_s[:, 2, :], start=True, stop=True).then_inc(s_t1, 1)
            pe.wait_ge(s_t1c, 1)
            nc.tensor.matmul(ps_h[:, 0:P], w0_s[:, 0, :], t1[:, :], start=True, stop=True).then_inc(s_wp, 1)
            pe.wait_ge(s_wpc, 1)
            pe.wait_ge(s_const, 9)

            def mul_w(g):
                pe.wait_ge(d_x[g], 16)
                if g >= 1:
                    pe.wait_ge(s_uc, g)
                if g >= 2:
                    pe.wait_ge(s_x1c, g - 1)
                for i in range(GB):
                    op = nc.tensor.matmul(ps_u[:, i * P:(i + 1) * P], x1T[:, g, i * P:(i + 1) * P], wp[:, :],
                                          start=True, stop=True)
                op.then_inc(s_u, 1)

            def rotate(g):
                pe.wait_ge(s_uc, g + 1)
                pe.wait_ge(s_rot, GB * (g + 1))
                if g >= 1:
                    pe.wait_ge(s_tanh, g)
                for i in range(GB):
                    op = nc.tensor.matmul(ps_h[:, i * P:(i + 1) * P], u[:, g % 2, i * P:(i + 1) * P],
                                          rot[:, g % 2, i, :], start=True, stop=True)
                op.then_inc(s_h, 1)

            def turn_x1(g):
                pe.wait_ge(s_x1T, g + 1)
                if g >= 1:
                    pe.wait_ge(s_x1c, g)
                pe.wait_ge(s_uc, min(g + 2, GROUPS))
                for i in range(GB):
                    op = nc.tensor.transpose(ps_x1[:, i * P:(i + 1) * P], x1T[:, g, i * P:(i + 1) * P], ident[:, :])
                op.then_inc(s_x1, 1)

            def down(g):
                pe.wait_ge(d_cond[g], 16 * GB)
                pe.wait_ge(s_x1T, g + 1)
                if g >= 1:
                    pe.wait_ge(s_zc, g)
                if g >= 4:
                    pe.wait_ge(s_nrc, g - 3)
                for b in range(g * GB, g * GB + GB):
                    op = nc.tensor.matmul(ps_z[:, cols(b)], cond_s[:, b, 0:P], x1T[:, g, cols(b)],
                                          start=True, stop=True)
                op.then_inc(s_z, 1)

            def up(g):
                pe.wait_ge(s_zc, g + 1)
                if g >= 1:
                    pe.wait_ge(s_yc, GB * g)
                for b in range(g * GB, g * GB + GB):
                    op = nc.tensor.matmul(ps_y[:, cols(b)], cond_s[:, b, P:2 * P], zT[:, g % 2, cols(b)],
                                          start=True, stop=True)
                op.then_inc(s_y, 1)

            def turn_y(g):
                pe.wait_ge(s_yc, GB * (g + 1))
                if g >= 2:
                    pe.wait_ge(s_yhat, g - 1)
                for i in range(GB):
                    op = nc.tensor.transpose(ps_yr[g % 2][:, i * P:(i + 1) * P], yT[:, g % 2, i * P:(i + 1) * P],
                                             ident[:, :])
                op.then_inc(s_yr, 1)

            def turn_yhat(g):
                pe.wait_ge(s_yhat, g + 1)
                if g >= 1:
                    pe.wait_ge(s_nTc, g)
                for i in range(GB):
                    op = nc.tensor.transpose(ps_n[:, i * P:(i + 1) * P], yhat[:, g % 2, i * P:(i + 1) * P],
                                             ident[:, :])
                op.then_inc(s_nT, 1)

            def route(g):
                pe.wait_ge(s_nTc, g + 1)
                if g >= 1:
                    pe.wait_ge(s_slot, g)
                for i in range(GB):
                    op = nc.tensor.matmul(ps_log[:, i * EXPERTS:(i + 1) * EXPERTS],
                                          xnT[:, g % 2, i * P:(i + 1) * P], wr_s[:, :], start=True, stop=True)
                op.then_inc(s_log, 1)
                pe.wait_ge(s_zc, min(g + 4, GROUPS))
                if g >= 1:
                    pe.wait_ge(s_nrc, g)
                for i in range(GB):
                    op = nc.tensor.transpose(ps_nr[:, i * P:(i + 1) * P], xnT[:, g % 2, i * P:(i + 1) * P],
                                             ident[:, :])
                op.then_inc(s_nr, 1)

            def prefix(g):
                pe.wait_ge(s_onehot, g + 1)
                pe.wait_ge(s_const, N_CONST)
                if g >= 1:
                    pe.wait_ge(s_slot, g)
                oh = onehot[:, g % 2, :, :].rearrange("p b e -> p (b e)")
                nc.tensor.matmul(ps_pre, before[:, :], oh, start=True, stop=False, skip_group_check=True)
                for back in range(1, GB):
                    n = (GB - back) * EXPERTS
                    nc.tensor.matmul(ps_pre[:, back * EXPERTS:], ones_b[:, :], oh[:, 0:n], start=False, stop=False,
                                     skip_group_check=True)
                pe.wait_ge(s_seen, g + 1)
                for i in range(GB):
                    op = nc.tensor.matmul(ps_pre[:, i * EXPERTS:(i + 1) * EXPERTS], ones_b[:, :],
                                          seen[:, g % 2, :], start=False, stop=(i == GB - 1),
                                          skip_group_check=True)
                if g in (SOONER - 1, GROUPS - 1):
                    pe.wait_ge(s_seen, g + 2)
                    op = nc.tensor.matmul(ps_cnt, ones_b[:, :], seen[:, (g + 1) % 2, :], start=True, stop=True,
                                          skip_group_check=True)
                op.then_inc(s_pre, 1)

            def turn_tile(k, arrivals):
                pe.wait_ge(d_rows[k], arrivals)
                nc.tensor.transpose(ps_t[:, k * P:(k + 1) * P], rows[:, k, 0:P], ident[:, :]).then_inc(s_tT, 1)

            def hidden(k, tiles_ready, read=None):
                pe.wait_ge(s_stage, tiles_ready)
                pe.wait_ge(s_tTc, tiles_ready)
                for half, used, done in ((ps_lo, s_hloc, s_hlo), (ps_hi, s_hhic, s_hhi)):
                    if read is not None:
                        pe.wait_ge(used, read)
                    for c in range(CHUNKS // 2) if half is ps_lo else range(CHUNKS // 2, CHUNKS):
                        op = nc.tensor.matmul(half[:, c * P:(c + 1) * P], stage[:, k, c * P:(c + 1) * P],
                                              tileT[:, k, :], start=True, stop=True)
                    op.then_inc(done, 1)

            def output(k, e, tiles_ready, freed=None):
                pe.wait_ge(s_hloc, tiles_ready)
                pe.wait_ge(s_hhic, tiles_ready)
                if freed is not None:
                    pe.wait_ge(s_res, freed)
                for c in range(CHUNKS):
                    w2_e = w2_s[:, bass.ds(e, 1), c, :].rearrange("p a d -> p (a d)")
                    op = nc.tensor.matmul(ps_out[k][:, 0:P], hT[:, k, c * P:(c + 1) * P], w2_e,
                                          start=(c == 0), stop=(c == CHUNKS - 1))
                op.then_inc(s_out, 1)

            pe.wait_ge(d_small, 48)
            steps = {"u": mul_w, "up": up, "h": rotate, "prefix": prefix, "yr": turn_y, "x1": turn_x1, "z": down,
                     "nT": turn_yhat, "route": route}
            for stage_name, g in in_turn({"up": 2, "u": 0, "nT": 4, "z": 1, "prefix": 5, "h": 0, "x1": 1, "yr": 2,
                                          "route": 4}):
                if (stage_name, g) == ("prefix", GROUPS - 3):
                    pe.wait_ge(s_tiles, 1)
                    pe.wait_ge(s_x1c, GROUPS)
                    turn_tile(0, 16)
                if (stage_name, g) == ("route", GROUPS - 2):
                    expert = loaded(PE, tile_e, 0, EXPERTS - 1)
                    pe.wait_ge(d_experts, 48)
                    hidden(0, 1)
                    turn_tile(1, 16)
                if (stage_name, g) == ("route", GROUPS - 1):
                    hidden(1, 2, 1)
                    turn_tile(2, 16)
                    output(0, expert[0], 1)
                if (stage_name, g) != ("prefix", GROUPS - 1):
                    steps[stage_name](g)
            hidden(2, 3, 2)
            turn_tile(0, 32)
            output(1, expert[1], 2)
            prefix(GROUPS - 1)
            hidden(0, 4, 3)
            turn_tile(1, 32)
            output(2, expert[2], 3)

            def tiles_between(first, last):
                with pe.Fori(first, last) as j:
                    for k in range(3):
                        hidden((k + 1) % 3, j * 3 + (k + 2), j * 3 + (k + 1))
                        turn_tile((k + 2) % 3, j * 16 + (16 if k == 0 else 32))
                        if k == 0:
                            expert = loaded(PE, tile_e, j * 3, EXPERTS - 1)
                        output(k, expert[k], j * 3 + (k + 1), j * 3 + (k - 2))

            tiles_between(1, SOON // 3)
            pe.wait_ge(s_experts, 1)
            tiles_between(SOON // 3, TILES // 3 - 1)
            expert = loaded(PE, tile_e, TILES - 3, EXPERTS - 1)
            hidden((TILES - 2) % 3, TILES - 1, TILES - 2)
            turn_tile((TILES - 1) % 3, 16 * (TILES // 3))
            output((TILES - 3) % 3, expert[0], TILES - 2, TILES - 5)
            hidden((TILES - 1) % 3, TILES, TILES - 1)
            output((TILES - 2) % 3, expert[1], TILES - 1, TILES - 4)
            output((TILES - 1) % 3, expert[2], TILES, TILES - 3)

        @block.vector
        def _(dve):
            def chained(counter, op, value):
                op.then_inc(counter, 1)
                dve.wait_ge(counter, value)

            dve.wait_ge(d_trig, 48)
            nc.vector.tensor_copy(amp_b, amp_s[:, 0:1].broadcast_to((P, BATCHES))).then_inc(s_chain, 1)
            chained(s_chain, nc.vector.tensor_scalar(ang, delta_s[:, :], freq_s[:, 0:1], None, ALU.mult), 2)
            chained(s_chain, nc.vector.tensor_scalar(turns, ang, 1.0 / (2 * 3.141592653589793), ROUND,
                                                     ALU.mult, ALU.add), 3)
            chained(s_chain, nc.vector.tensor_scalar(turns, turns, ROUND, None, ALU.subtract), 4)
            chained(s_chain, nc.vector.scalar_tensor_tensor(out=red, in0=turns, scalar=-TWO_PI_A, in1=ang,
                                                            op0=ALU.mult, op1=ALU.add), 5)
            chained(s_chain, nc.vector.scalar_tensor_tensor(out=ang, in0=turns, scalar=-TWO_PI_B, in1=red,
                                                            op0=ALU.mult, op1=ALU.add), 6)
            nc.vector.scalar_tensor_tensor(out=red, in0=turns, scalar=-TWO_PI_C, in1=ang,
                                           op0=ALU.mult, op1=ALU.add).then_inc(s_red, 1)
            dve.wait_ge(s_red, 1)
            nc.vector.tensor_scalar(red, red, -PI_DOWN, PI_DOWN, ALU.max, ALU.min).then_inc(s_red, 1)
            dve.wait_ge(s_red, 2)
            nc.vector.tensor_scalar(turns, red, -1.0, None, ALU.mult).then_inc(s_red, 1)
            dve.wait_ge(s_red, 3)
            nc.vector.tensor_tensor(ang, red, turns, ALU.max).then_inc(s_red, 1)
            dve.wait_ge(s_red, 4)
            nc.vector.tensor_scalar(cosr, ang, -1.0, 1.5707963267948966, ALU.mult, ALU.add).then_inc(s_chain, 1)
            dve.wait_ge(s_sin, 2)

            def tables(n, part):
                dve.wait_ge(s_amp, n)
                nc.vector.tensor_tensor(cs[:, 0, part], cos_t[:, part], amp_t[:, part], ALU.mult)\
                    .then_inc(s_chain, 1)
                nc.vector.tensor_tensor(cs[:, 1, part], sin_t[:, part], amp_t[:, part], ALU.mult)\
                    .then_inc(s_chain, 1)

            tables(1, PARTS[0])
            tables(2, PARTS[1])
            nc.vector.memset(seen[:, 0, :], 0.0).then_inc(s_seen, 1)
            dve.wait_ge(s_chain, 9)

            def build_rot(g, i):
                if i == 0:
                    dve.wait_ge(s_rotc, g + 1)
                    if g >= 2:
                        dve.wait_ge(s_h, g - 1)
                b = g * GB + i
                nc.vector.scalar_tensor_tensor(out=rot[:, g % 2, i, :], in0=swap[:, :],
                                               scalar=cs[:, 1, b:b + 1], in1=rot_c[:, g % 2, i, :],
                                               op0=ALU.mult, op1=ALU.add).then_inc(s_rot, 1)

            def add_y(g, i):
                if i == 0:
                    dve.wait_ge(d_cond[g], 16 * GB)
                    dve.wait_ge(s_y, g + 1)
                    if g >= 2:
                        dve.wait_ge(s_yr, g - 1)
                b = g * GB + i
                nc.vector.scalar_tensor_tensor(out=yT[:, g % 2, cols(b)], in0=ps_y[:, cols(b)],
                                               scalar=cond_s[:, b, 2 * P + 1:2 * P + 2],
                                               in1=x1T[:, g, cols(b)], op0=ALU.add, op1=ALU.add).then_inc(s_yc, 1)

            def moments(g):
                dve.wait_ge(s_yr, g + 1)
                for i in range(GB):
                    nc.vector.bn_stats(stats[:, g % 2, i, :], ps_yr[g % 2][:, i * P:(i + 1) * P])\
                        .then_inc(s_stats, 1)
                for i in range(GB):
                    dve.wait_ge(s_stats, GB * g + i + 1)
                    op = nc.vector.bn_aggr(mv[:, g % 2, i, :], stats[:, g % 2, i, :])
                op.then_inc(s_mv, 1)

            def add_eps(g):
                dve.wait_ge(s_mv, g + 1)
                nc.vector.tensor_scalar(vareps[:, g % 2, :], mv[:, g % 2, :, 1], EPS, None, ALU.add)\
                    .then_inc(s_var, 1)

            def normalise(g):
                dve.wait_ge(s_rstd, g + 1)
                if g >= 2:
                    dve.wait_ge(s_nT, g - 1)
                for i in range(GB):
                    op = nc.vector.tensor_scalar(yhat[:, g % 2, i * P:(i + 1) * P],
                                                 ps_yr[g % 2][:, i * P:(i + 1) * P],
                                                 mv[:, g % 2, i, 0:1], rstd[:, g % 2, i:i + 1],
                                                 ALU.subtract, ALU.mult)
                op.then_inc(s_yhat, 1)

            def wide(t):
                return t.unsqueeze(2).broadcast_to((P, GB, EXPERTS))

            def pick(g, part):
                if part == 0:
                    dve.wait_ge(s_log, g + 1)
                    if g >= 2:
                        dve.wait_ge(s_pre, g - 1)
                    nc.vector.tensor_tensor(logits[:, :, :], ps_log.rearrange("p (b e) -> p b e", b=GB),
                                            br_s[:, :].unsqueeze(1).broadcast_to((P, GB, EXPERTS)),
                                            ALU.add).then_inc(s_pick, 1)
                    return
                dve.wait_ge(s_pick, PICKS * g + part)
                if part == 1:
                    op = nc.vector.tensor_reduce(top[:, :], logits[:, :, :], AX.X, ALU.max)
                elif part == 2:
                    op = nc.vector.tensor_tensor(tied[:, :, :], logits[:, :, :], wide(top[:, :]), ALU.is_equal)
                elif part == 3:
                    op = nc.vector.tensor_tensor(tied[:, :, :], tied[:, :, :], falling[:, :, :], ALU.mult)
                elif part == 4:
                    op = nc.vector.tensor_reduce(first[:, :], tied[:, :, :], AX.X, ALU.max)
                elif part == 5:
                    op = nc.vector.tensor_tensor(onehot[:, g % 2, :, :], falling[:, :, :], wide(first[:, :]),
                                                 ALU.is_equal)
                    op.then_inc(s_onehot, 1)
                    return
                op.then_inc(s_pick, 1)

            def count(g, part):
                if part == 0:
                    dve.wait_ge(s_onehot, g + 1)
                    nc.vector.tensor_reduce(groupsum[:, :], onehot[:, g % 2, :, :].rearrange("p b e -> p e b"),
                                            AX.X, ALU.add).then_inc(s_groupsum, 1)
                else:
                    dve.wait_ge(s_groupsum, g + 1)
                    nc.vector.tensor_tensor(seen[:, (g + 1) % 2, :], seen[:, g % 2, :], groupsum[:, :], ALU.add)\
                        .then_inc(s_seen, 1)

            def find_slot(g, part):
                if part == 0:
                    dve.wait_ge(s_pre, g + 1)
                    if g == SOONER - 1:
                        nc.vector.tensor_copy(cnt_i[:, :], ps_cnt[0:1, :]).then_inc(s_counted, 1)
                    nc.vector.tensor_tensor(place[:, :, :], ps_pre.rearrange("p (b e) -> p b e", b=GB),
                                            area[:, :].unsqueeze(1).broadcast_to((P, GB, EXPERTS)),
                                            ALU.add).then_inc(s_place, 1)
                elif part == 1:
                    dve.wait_ge(s_place, 2 * g + 1)
                    nc.vector.tensor_tensor(place[:, :, :], place[:, :, :], onehot[:, g % 2, :, :], ALU.mult)\
                        .then_inc(s_place, 1)
                else:
                    dve.wait_ge(s_place, 2 * g + 2)
                    with nc.allow_low_precision(reason="row numbers are integers below 2**24"):
                        nc.vector.tensor_reduce(slot[:, g * GB:(g + 1) * GB], place[:, :, :], AX.X, ALU.add)\
                            .then_inc(s_slot, 1)

            tabled = [0]

            def table(op):
                tabled[0] += 1
                op.then_inc(s_table, 1)

            def tabled_but(n):
                dve.wait_ge(s_table, tabled[0] - n)

            def running_sum():
                table(nc.vector.tensor_tensor_scan(cum[:, :], ones_8[:, :], nt[:, :], 0.0, ALU.mult, ALU.add))

            def is_past(n):
                table(nc.vector.tensor_tensor(past[:, 0:n, :], cum[:, :].unsqueeze(1).broadcast_to((1, n, EXPERTS)),
                                              tau[:, 0:n].unsqueeze(2).broadcast_to((1, n, EXPERTS)), ALU.is_le))

            def experts_past(n):
                table(nc.vector.tensor_reduce(esum[:, 0:n], past[:, 0:n, :], AX.X, ALU.add))

            def experts_of(first, n):
                table(nc.vector.tensor_scalar(tile_e[:, first:first + n], esum[:, 0:n], float(EXPERTS - 1), None,
                                              ALU.min))

            def jumps(n):
                table(nc.vector.tensor_tensor(pastw[:, 0:n, :], past[:, 0:n, :],
                                              jump[:, :].unsqueeze(1).broadcast_to((1, n, EXPERTS)), ALU.mult))

            def jumped(n):
                table(nc.vector.tensor_reduce(tsum[:, 0:n], pastw[:, 0:n, :], AX.X, ALU.add))

            def sooner_tiles(part):
                if part == 0:
                    dve.wait_ge(s_counted, 1)
                    table(nc.vector.memset(capped[:, 0:1], 0.0))
                    table(nc.vector.memset(taken[:, EXPERTS:], 0.0))
                    table(nc.vector.tensor_scalar(nt_i[:, :], cnt_i[:, :], 7, None, ALU.logical_shift_right))
                elif part == 1:
                    tabled_but(0)
                    table(nc.vector.tensor_copy(nt[:, :], nt_i[:, :]))
                elif part == 2:
                    tabled_but(0)
                    table(nc.vector.tensor_scalar(jump[:, :], nt[:, :], -float(P), float(PITCH), ALU.mult,
                                                  ALU.add))
                    running_sum()
                elif part == 3:
                    tabled_but(0)
                    table(nc.vector.tensor_scalar(capped[:, 1:], cum[:, :], float(SOON), None, ALU.min))
                    is_past(SOON)
                elif part == 4:
                    tabled_but(0)
                    table(nc.vector.tensor_tensor(taken[:, 0:EXPERTS], capped[:, 1:], capped[:, 0:EXPERTS],
                                                  ALU.subtract))
                    jumps(SOON)
                    experts_past(SOON)
                elif part == 5:
                    tabled_but(0)
                    table(nc.vector.tensor_tensor(step_up[:, :], taken[:, 1:], taken[:, 0:EXPERTS], ALU.subtract))
                    jumped(SOON)
                    experts_of(0, SOON)
                elif part == 6:
                    tabled_but(0)
                    table(nc.vector.tensor_scalar(taken_0[:, :], taken[:, 0:1], float(P), None, ALU.mult))
                    table(nc.vector.tensor_scalar(step_up[:, :], step_up[:, :], float(P), float(PITCH), ALU.mult,
                                                  ALU.add))
                    nc.vector.tensor_tensor(tile_r[:, 0:SOON], tsum[:, 0:SOON], tau128[:, 0:SOON], ALU.add)\
                        .then_inc(s_tiles, 1)

            def later_tiles(part):
                tabled_but(0)
                if part == 0:
                    table(nc.vector.tensor_scalar(cnt_i[:, :], ps_cnt[0:1, :], float(P - 1), None, ALU.add))
                elif part == 1:
                    table(nc.vector.tensor_scalar(nt_i[:, :], cnt_i[:, :], 7, None, ALU.logical_shift_right))
                elif part == 2:
                    table(nc.vector.tensor_tensor(nt[:, :], nt_i[:, :], taken[:, 0:EXPERTS], ALU.subtract))
                elif part == 3:
                    table(nc.vector.scalar_tensor_tensor(out=jump[:, :], in0=nt[:, :], scalar=-float(P),
                                                         in1=step_up[:, :], op0=ALU.mult, op1=ALU.add))
                    running_sum()
                elif part == 4:
                    is_past(LATER)
                elif part == 5:
                    jumps(LATER)
                elif part == 6:
                    jumped(LATER)
                elif part == 7:
                    table(nc.vector.scalar_tensor_tensor(out=tsum[:, 0:LATER], in0=tsum[:, 0:LATER],
                                                         scalar=taken_0[:, 0:1], in1=tau128[:, 0:LATER],
                                                         op0=ALU.add, op1=ALU.add))
                elif part == 8:
                    nc.vector.tensor_scalar(tile_r[:, SOON:TILES], tsum[:, 0:LATER], float(DUMMY), None, ALU.min)\
                        .then_inc(s_tiles, 1)
                elif part == 9:
                    experts_past(LATER)
                else:
                    nc.vector.tensor_scalar(tile_e[:, SOON:TILES], esum[:, 0:LATER], float(EXPERTS - 1), None,
                                            ALU.min).then_inc(s_experts, 1)

            def stage_expert(k, e):
                nc.vector.tensor_scalar(stage[:, k, :], w1_s[:, bass.ds(e, 1), :].rearrange("p a f -> p (a f)"),
                                        1.0, None, ALU.mult).then_inc(s_stage, 1)

            def residual(k, arrivals, staged, freed=None):
                dve.wait_ge(d_rows[k], arrivals)
                dve.wait_ge(s_stage, staged)
                if freed is not None:
                    dve.wait_ge(s_res, freed)
                nc.vector.tensor_tensor(resid[:, k, :], rows[:, k, P:2 * P], stage[:, k, EB:EW], ALU.add)\
                    .then_inc(s_resid, 1)

            def relu_hi(k, tiles_done):
                dve.wait_ge(s_hhi, tiles_done)
                for c in range(CHUNKS // 2, CHUNKS):
                    op = nc.vector.tensor_scalar(hT[:, k, c * P:(c + 1) * P], ps_hi[:, c * P:(c + 1) * P],
                                                 stage[:, k, FF + c:FF + c + 1], 0.0, ALU.add, ALU.max)
                op.then_inc(s_hhic, 1)

            def front_step(t, between=lambda part: None):
                routed, added, built, normed = t - 5, t - 2, t + 1, t - 3
                routing, adding = 0 <= routed < GROUPS, 0 <= added < GROUPS
                building, norming = 0 <= built < GROUPS, 0 <= normed < GROUPS
                if norming:
                    moments(normed)
                if routing:
                    if routed == 0:
                        dve.wait_ge(s_const, N_CONST)
                        dve.wait_ge(d_small, 48)
                    pick(routed, 0)
                if norming:
                    add_eps(normed)
                for part in range(1, 6):
                    if routing:
                        pick(routed, part)
                    between(part - 1)
                    if adding and part < 5:
                        add_y(added, part - 1)
                if built == 2:
                    tables(3, PARTS[2])
                if building:
                    dve.wait_ge(s_chain, 9 if built < 2 else 11 if built < 4 else 13)
                    build_rot(built, 0)
                if routing:
                    count(routed, 0)
                between(5)
                if building:
                    build_rot(built, 1)
                if routing:
                    count(routed, 1)
                between(6)
                if building:
                    build_rot(built, 2)
                    build_rot(built, 3)
                if routing and routed < GROUPS - 2:
                    for part in range(3):
                        find_slot(routed, part)
                if norming:
                    normalise(normed)

            def result(k, tiles_done, stored=None):
                dve.wait_ge(s_out, tiles_done)
                dve.wait_ge(s_resid, tiles_done)
                if stored is not None:
                    dve.wait_ge(d_res[k], stored)
                nc.vector.tensor_tensor(res[:, k, :], ps_out[k][:, 0:P], resid[:, k, :], ALU.add)\
                    .then_inc(s_res, 1)

            def step(t, e, between=lambda i: None):
                relu_hi(t % 3, t + 1)
                between(0)
                if e is not None:
                    dve.wait_ge(s_hloc, t + 1)
                    dve.wait_ge(s_hhic, t + 1)
                    dve.wait_ge(s_resid, t + 1)
                    stage_expert(t % 3, e)
                between(1)
                if t >= 1:
                    result((t - 1) % 3, t, 16 * ((t - 1) // 3) if t > 3 else None)
                between(2)
                if t + 1 < TILES:
                    residual((t + 1) % 3, 16 * ((t + 1) // 3 + 1), t + 2, t - 1 if t >= 2 else None)

            dve.wait_ge(s_const, 9)
            for i in range(GB):
                build_rot(0, i)
            for t in range(SOONER + 5):
                front_step(t)
            front_step(SOONER + 5, sooner_tiles)
            dve.wait_ge(s_tiles, 1)
            dve.wait_ge(d_experts, 48)
            expert = loaded(DVE, tile_e, 0, EXPERTS - 1)
            front_step(SOONER + 6, lambda part: stage_expert(part, expert[part]) if part < 3 else None)
            assert SOONER + 7 == GROUPS + 3

            expert = loaded(DVE, tile_e, 3, EXPERTS - 1)
            residual(0, 16, 1)
            step(0, expert[0])
            front_step(GROUPS + 3)
            for part in range(3):
                find_slot(GROUPS - 2, part)
            step(1, expert[1])
            front_step(GROUPS + 4)
            step(2, expert[2])
            for part in range(3):
                find_slot(GROUPS - 1, part)
            nc.vector.tensor_tensor(pad_row[:, :], ps_cnt[0:1, :], area[0:1, :], ALU.add).then_inc(s_padrow, 1)
            for part in range(4):
                later_tiles(part)
            expert = loaded(DVE, tile_e, 6, EXPERTS - 1)
            step(3, expert[0], lambda i: later_tiles(4 + i))
            step(4, expert[1], lambda i: later_tiles(7 + i) if i < 2 else None)
            step(5, expert[2], lambda i: later_tiles(9 + i) if i < 2 else None)
            dve.wait_ge(s_experts, 1)
            step(6, loaded(DVE, tile_e, 9, EXPERTS - 1)[0])
            with dve.Fori(2, TILES // 3 - 2) as j:
                for k in range(3):
                    relu_hi((k + 1) % 3, j * 3 + (k + 2))
                    if k == 0:
                        expert = loaded(DVE, tile_e, j * 3 + 4, EXPERTS - 1)
                    dve.wait_ge(s_hloc, j * 3 + (k + 2))
                    dve.wait_ge(s_hhic, j * 3 + (k + 2))
                    dve.wait_ge(s_resid, j * 3 + (k + 2))
                    stage_expert((k + 1) % 3, expert[k])
                    result(k, j * 3 + (k + 1), j * 16)
                    residual((k + 2) % 3, j * 16 + (16 if k == 0 else 32), j * 3 + (k + 3), j * 3 + k)
            last = loaded(DVE, tile_e, TILES - 3, EXPERTS - 1)[1:]
            for t in range(TILES - 5, TILES):
                step(t, last[t - TILES + 5] if t < TILES - 3 else None)
            result((TILES - 1) % 3, TILES, 16 * ((TILES - 1) // 3))


def kernel(**inputs):
    import numpy as np
    import concourse.bacc as _bacc
    from concourse import mybir as _mybir
    from concourse.bass_utils import run_bass_kernel_spmd as _run

    a = {k: np.asarray(v) for k, v in inputs.items()}
    laid = {
        "xT": a["x"].transpose(2, 0, 1).reshape(P, TOKENS),
        "w0": np.stack([a["L0_ffn_weight"].T, a["L0_ffn_aux_weight1"].T, a["L0_ffn_aux_weight2"]], axis=1),
        "bias0": a["L0_ffn_bias"],
        "amp": np.repeat(a["L0_cond_amplitudes"], 2),
        "freq": np.repeat(a["L0_cond_frequencies"], 2),
        "delta": a["condB_deltat"],
        "prof": a["itok_B_0_6"],
        "cond": np.concatenate([a["L1_cond_down_w"], a["L1_cond_up_w"], a["L1_cond_down_b"][:, :, None],
                                a["L1_cond_up_b"][:, :, None], a["L1_cond_ln_g"][:, :, None],
                                a["L1_cond_ln_b"][:, :, None]], axis=2),
        "wr": a["L1_ffn_Wr"].T,
        "br": a["L1_ffn_br"],
        "w1": np.concatenate([a["L1_ffn_W1"].transpose(2, 0, 1),
                              a["L1_ffn_b1"].reshape(EXPERTS, CHUNKS, P).transpose(2, 0, 1)], axis=2),
        "w2": a["L1_ffn_W2"].reshape(EXPERTS, P, CHUNKS, P).transpose(3, 0, 2, 1),
        "b2": a["L1_ffn_b2"],
    }
    nc = _bacc.Bacc("TRN2", target_bir_lowering=False, num_devices=1)
    arrays, args = {}, []
    for name, v in laid.items():
        v = np.ascontiguousarray(v)
        arrays[f"in_{name}"] = v
        args.append(nc.dram_tensor(f"in_{name}", v.shape, _mybir.dt.from_np(v.dtype), kind="ExternalInput").ap())
    args.append(nc.dram_tensor("out_0", (BATCHES, P, P), _mybir.dt.float32, kind="ExternalOutput").ap())
    adaln_moe(nc, *args)
    r = _run(nc, [arrays], core_ids=[0])
    return r.results[0]["out_0"]
```
